# Optimizing a Trainium2 kernel written in Bass

```python
import numpy as np
import jax
import jax.numpy as jnp

def _softmax(x, axis=-1):
    return jax.nn.softmax(x, axis=axis)

def _gelu(x):
    return jax.nn.gelu(x, approximate=True)

def _silu(x):
    return jax.nn.silu(x)

def _sigmoid(x):
    return jax.nn.sigmoid(x)

def _layernorm(x, axis=-1, eps=1e-05):
    m = jnp.mean(x, axis=axis, keepdims=True)
    v = jnp.var(x, axis=axis, keepdims=True)
    return (x - m) / jnp.sqrt(v + eps)

def _scatter_add(tgt, idx, src, axis=0):
    return tgt.at[idx].add(src)

def _segment_sum(src, seg, n):
    return jax.ops.segment_sum(src, seg, n)
kernel_name = 'mk_flamingo_gated_d2_seqx_r4_6bc519'

def setup_inputs(seed: int=0):
    np.random.seed(seed)
    _w = jnp.asarray

    def _rec_inputs():
        import jax
        import jax.numpy as jnp
        _rk = jax.random.key(seed)
        x = -0.0002928 + 1 * jax.random.normal(jax.random.fold_in(_rk, 1), (8, 512, 256), jnp.float32)
        _lenS = 512 - jax.random.randint(jax.random.fold_in(_rk, 7), (8,), 0, max(1, 512 // 4) + 1, jnp.int32)
        _lenS2 = 512 - jax.random.randint(jax.random.fold_in(_rk, 8), (8,), 0, max(1, 512 // 4) + 1, jnp.int32)
        _ctx_1024P = jax.random.normal(jax.random.fold_in(_rk, 11), (8, 16, 256), jnp.float32)
        _ctx_1024c = jax.random.dirichlet(jax.random.fold_in(_rk, 511), 0.3 * jnp.ones((16,), jnp.float32), (8, 512))
        _ctx_1024t = jnp.einsum('bsk,bkd->bsd', _ctx_1024c, _ctx_1024P)
        _ctx_1024t = _ctx_1024t * jax.lax.rsqrt(jnp.mean(jnp.square(_ctx_1024t)) + 1e-12) * 0.953939
        ctx_1024 = -1.39393e-06 + 0.999914 * (_ctx_1024t + 0.3 * jax.random.normal(jax.random.fold_in(_rk, 611), (8, 512, 256), jnp.float32))
        fside_BxSx4_0 = jax.random.uniform(jax.random.fold_in(_rk, 12), (8, 512, 4), jnp.float32, 0.0, 0.999884)
        _g = jax.random.normal(jax.random.fold_in(_rk, 9001), (2, 2), jnp.float32)
        _g = jnp.sign(_g) * jnp.maximum(jnp.abs(_g), 1.0) + (_g == 0) * 1.0
        g_xattn = _g[0]
        g_ffn = _g[1]
        return (x, ctx_1024, fside_BxSx4_0, g_xattn, g_ffn)
    x, ctx_1024, fside_BxSx4_0, g_xattn, g_ffn = _rec_inputs()

    def _L0_xattn_setup():
        import jax, jax.numpy as jnp
        import numpy as np
        D_MODEL = 256
        H = 16
        D_K = 64
        D_V = 64
        D_G = D_MODEL // H
        WAVE_LEN = 1000.0
        B = 8
        N = 128

        def box_relational_embedding(boxes, dim_g=D_G):
            x_min, y_min, x_max, y_max = jnp.split(boxes, 4, axis=-1)
            cx = (x_min + x_max) * 0.5
            cy = (y_min + y_max) * 0.5
            w = x_max - x_min + 1.0
            h = y_max - y_min + 1.0
            delta_x = jnp.log(jnp.clip(jnp.abs((cx - jnp.swapaxes(cx, 1, 2)) / w), 0.001, None))
            delta_y = jnp.log(jnp.clip(jnp.abs((cy - jnp.swapaxes(cy, 1, 2)) / h), 0.001, None))
            delta_w = jnp.log(w / jnp.swapaxes(w, 1, 2))
            delta_h = jnp.log(h / jnp.swapaxes(h, 1, 2))
            pos = jnp.stack([delta_x, delta_y, delta_w, delta_h], axis=-1)
            n_freq = dim_g // 8
            feat_range = jnp.arange(n_freq, dtype=jnp.float32)
            dim_mat = 1.0 / WAVE_LEN ** (feat_range / n_freq)
            mul = (100.0 * pos)[..., None] * dim_mat
            b, n = (pos.shape[0], pos.shape[1])
            mul = mul.reshape(b, n, n, 4 * n_freq)
            return jnp.concatenate([jnp.sin(mul), jnp.cos(mul)], axis=-1)
        key = jax.random.key(seed)
        ks = jax.random.split(key, 12)
        s = 0.02
        inp = {'queries': jax.random.normal(ks[0], (B, N, D_MODEL), jnp.float32), 'keys': jax.random.normal(ks[1], (B, N, D_MODEL), jnp.float32), 'values': jax.random.normal(ks[2], (B, N, D_MODEL), jnp.float32), 'boxes': jax.random.uniform(ks[3], (B, N, 4), jnp.float32), 'Wq': jax.random.normal(ks[4], (H * D_K, D_MODEL), jnp.float32) * s, 'bq': jnp.zeros((H * D_K,), jnp.float32), 'Wk': jax.random.normal(ks[5], (H * D_K, D_MODEL), jnp.float32) * s, 'bk': jnp.zeros((H * D_K,), jnp.float32), 'Wv': jax.random.normal(ks[6], (H * D_V, D_MODEL), jnp.float32) * s, 'bv': jnp.zeros((H * D_V,), jnp.float32), 'Wo': jax.random.normal(ks[7], (D_MODEL, H * D_V), jnp.float32) * s, 'bo': jnp.zeros((D_MODEL,), jnp.float32), 'Wg': jax.random.normal(ks[8], (H, D_G), jnp.float32) * s, 'bg': jnp.zeros((H,), jnp.float32)}
        return inp
    _L0_xattn_all = _L0_xattn_setup()
    _L0_xattn_in = {k: v for k, v in _L0_xattn_all.items() if k in ('Wq', 'bq', 'Wk', 'bk', 'Wv', 'bv', 'Wo', 'bo', 'Wg', 'bg')}
    del _L0_xattn_all

    def _L0_ffn_setup():
        import jax, jax.numpy as jnp
        import numpy as np
        D = 256
        H = 4
        HD = D // H
        E = 8
        FF = 1024
        CAP_FACTOR = 1.0

        def _ln(x, g, b, eps=1e-05):
            mu = jnp.mean(x, -1, keepdims=True)
            v = jnp.mean((x - mu) ** 2, -1, keepdims=True)
            return (x - mu) * jax.lax.rsqrt(v + eps) * g + b

        def _mha(x, w, b, ow, ob):
            L, N, _ = x.shape
            qkv = x @ w.T + b
            q, k, v = jnp.split(qkv, 3, axis=-1)
            rh = lambda t: t.reshape(L, N, H, HD).transpose(1, 2, 0, 3)
            q, k, v = (rh(q), rh(k), rh(v))
            scores = jnp.einsum('nhld,nhmd->nhlm', q, k) / np.float32(np.sqrt(HD))
            attn = jax.nn.softmax(scores, axis=-1)
            o = jnp.einsum('nhlm,nhmd->nhld', attn, v).transpose(2, 0, 1, 3).reshape(L, N, D)
            return o @ ow.T + ob

        def _moe(x, wg, w1, b1, w2, b2):
            L, N, _ = x.shape
            S = L * N
            cap = int(CAP_FACTOR * S) // E
            xf = x.reshape(S, D)
            gates = jax.nn.softmax(xf @ wg, axis=-1)
            idx = jnp.argmax(gates, axis=-1)
            mask1 = jax.nn.one_hot(idx, E, dtype=x.dtype)
            loc = jnp.sum((jnp.cumsum(mask1, 0) - 1.0) * mask1, -1).astype(jnp.int32)
            keep = loc < cap
            gate_val = jnp.take_along_axis(gates, idx[:, None], -1)[:, 0]
            slot = jnp.where(keep, idx.astype(jnp.int32) * cap + loc, E * cap)
            disp = jnp.zeros((E * cap, D), x.dtype).at[slot].set(xf, mode='drop')
            disp = disp.reshape(E, cap, D)
            h = jnp.einsum('ecd,edf->ecf', disp, w1) + b1[:, None, :]
            y = (jnp.einsum('ecf,efd->ecd', h, w2) + b2[:, None, :]).reshape(E * cap, D)
            out = jnp.where(keep[:, None], gate_val[:, None] * y[jnp.minimum(slot, E * cap - 1)], 0.0)
            return out.reshape(L, N, D)
        key = jax.random.key(seed)
        ks = jax.random.split(key, 8)
        L, N = (256, 16)
        s = 0.02
        return {'x': jax.random.normal(ks[0], (L, N, D), jnp.float32), 'in_proj_w': jax.random.normal(ks[1], (3 * D, D), jnp.float32) * s, 'in_proj_b': jnp.zeros((3 * D,), jnp.float32), 'out_proj_w': jax.random.normal(ks[2], (D, D), jnp.float32) * s, 'out_proj_b': jnp.zeros((D,), jnp.float32), 'ln1_g': jnp.ones((D,), jnp.float32), 'ln1_b': jnp.zeros((D,), jnp.float32), 'ln2_g': jnp.ones((D,), jnp.float32), 'ln2_b': jnp.zeros((D,), jnp.float32), 'wg': jax.random.normal(ks[3], (D, E), jnp.float32) * s, 'w1': jax.random.normal(ks[4], (E, D, FF), jnp.float32) * s, 'b1': jnp.zeros((E, FF), jnp.float32), 'w2': jax.random.normal(ks[5], (E, FF, D), jnp.float32) * s, 'b2': jnp.zeros((E, D), jnp.float32)}
    _L0_ffn_all = _L0_ffn_setup()
    _L0_ffn_in = {k: v for k, v in _L0_ffn_all.items() if k in ('in_proj_w', 'in_proj_b', 'out_proj_w', 'out_proj_b', 'ln1_g', 'ln1_b', 'ln2_g', 'ln2_b', 'wg', 'w1', 'b1', 'w2', 'b2')}
    del _L0_ffn_all

    def _L1_xattn_setup():
        import jax, jax.numpy as jnp
        import numpy as np
        D = 256
        H = 8
        B, S = (4, 512)
        key = jax.random.key(seed)
        ks = jax.random.split(key, 11)
        s = 0.02
        return {'Q': jax.random.normal(ks[0], (B, S, D), jnp.float32), 'K': jax.random.normal(ks[1], (B, S, D), jnp.float32), 'V': jax.random.normal(ks[2], (B, S, D), jnp.float32), 'WQ': jax.random.normal(ks[3], (D, D), jnp.float32) * s, 'bQ': jax.random.normal(ks[4], (D,), jnp.float32) * s, 'WK': jax.random.normal(ks[5], (D, D), jnp.float32) * s, 'bK': jax.random.normal(ks[6], (D,), jnp.float32) * s, 'WV': jax.random.normal(ks[7], (D, D), jnp.float32) * s, 'bV': jax.random.normal(ks[8], (D,), jnp.float32) * s, 'Wl': jax.random.normal(ks[9], (D, D * H), jnp.float32) * s, 'bl': jax.random.normal(ks[10], (D,), jnp.float32) * s}
    _L1_xattn_all = _L1_xattn_setup()
    _L1_xattn_in = {k: v for k, v in _L1_xattn_all.items() if k in ('WQ', 'bQ', 'WK', 'bK', 'WV', 'bV', 'Wl', 'bl')}
    del _L1_xattn_all

    def _L1_ffn_setup():
        import jax, jax.numpy as jnp
        import numpy as np
        import math
        BETA = 0.9
        THRESHOLD = 1.0
        NUM_STEPS = 5
        ALPHA = 2.0

        @jax.custom_vjp
        def spike_fn(u):
            return (u > 0).astype(u.dtype)

        def _spike_fwd(u):
            return (spike_fn(u), u)

        def _spike_bwd(u, g):
            s = jnp.pi / 2.0 * ALPHA * u
            return (g * (ALPHA / 2.0) / (1.0 + s * s),)
        spike_fn.defvjp(_spike_fwd, _spike_bwd)
        key = jax.random.key(seed)
        k1, k2, k3 = jax.random.split(key, 3)
        n_embd = 256
        x = jax.random.normal(k1, (4, 512, n_embd), dtype=jnp.float32)
        W_fc = jax.random.normal(k2, (4 * n_embd, n_embd), dtype=jnp.float32) / math.sqrt(n_embd)
        W_proj = jax.random.normal(k3, (n_embd, 4 * n_embd), dtype=jnp.float32) / math.sqrt(4 * n_embd)
        return {'x': x, 'W_fc': W_fc, 'W_proj': W_proj}
    _L1_ffn_all = _L1_ffn_setup()
    _L1_ffn_in = {k: v for k, v in _L1_ffn_all.items() if k in ('W_fc', 'W_proj')}
    del _L1_ffn_all
    return {'x': x, 'ctx_1024': ctx_1024, 'fside_BxSx4_0': fside_BxSx4_0, 'g_xattn': g_xattn, 'g_ffn': g_ffn, 'L0_xattn_Wq': _L0_xattn_in['Wq'], 'L0_xattn_bq': _L0_xattn_in['bq'], 'L0_xattn_Wk': _L0_xattn_in['Wk'], 'L0_xattn_bk': _L0_xattn_in['bk'], 'L0_xattn_Wv': _L0_xattn_in['Wv'], 'L0_xattn_bv': _L0_xattn_in['bv'], 'L0_xattn_Wo': _L0_xattn_in['Wo'], 'L0_xattn_bo': _L0_xattn_in['bo'], 'L0_xattn_Wg': _L0_xattn_in['Wg'], 'L0_xattn_bg': _L0_xattn_in['bg'], 'L0_ffn_in_proj_w': _L0_ffn_in['in_proj_w'], 'L0_ffn_in_proj_b': _L0_ffn_in['in_proj_b'], 'L0_ffn_out_proj_w': _L0_ffn_in['out_proj_w'], 'L0_ffn_out_proj_b': _L0_ffn_in['out_proj_b'], 'L0_ffn_ln1_g': _L0_ffn_in['ln1_g'], 'L0_ffn_ln1_b': _L0_ffn_in['ln1_b'], 'L0_ffn_ln2_g': _L0_ffn_in['ln2_g'], 'L0_ffn_ln2_b': _L0_ffn_in['ln2_b'], 'L0_ffn_wg': _L0_ffn_in['wg'], 'L0_ffn_w1': _L0_ffn_in['w1'], 'L0_ffn_b1': _L0_ffn_in['b1'], 'L0_ffn_w2': _L0_ffn_in['w2'], 'L0_ffn_b2': _L0_ffn_in['b2'], 'L1_xattn_WQ': _L1_xattn_in['WQ'], 'L1_xattn_bQ': _L1_xattn_in['bQ'], 'L1_xattn_WK': _L1_xattn_in['WK'], 'L1_xattn_bK': _L1_xattn_in['bK'], 'L1_xattn_WV': _L1_xattn_in['WV'], 'L1_xattn_bV': _L1_xattn_in['bV'], 'L1_xattn_Wl': _L1_xattn_in['Wl'], 'L1_xattn_bl': _L1_xattn_in['bl'], 'L1_ffn_W_fc': _L1_ffn_in['W_fc'], 'L1_ffn_W_proj': _L1_ffn_in['W_proj']}

def reference(x, ctx_1024, fside_BxSx4_0, g_xattn, g_ffn, L0_xattn_Wq, L0_xattn_bq, L0_xattn_Wk, L0_xattn_bk, L0_xattn_Wv, L0_xattn_bv, L0_xattn_Wo, L0_xattn_bo, L0_xattn_Wg, L0_xattn_bg, L0_ffn_in_proj_w, L0_ffn_in_proj_b, L0_ffn_out_proj_w, L0_ffn_out_proj_b, L0_ffn_ln1_g, L0_ffn_ln1_b, L0_ffn_ln2_g, L0_ffn_ln2_b, L0_ffn_wg, L0_ffn_w1, L0_ffn_b1, L0_ffn_w2, L0_ffn_b2, L1_xattn_WQ, L1_xattn_bQ, L1_xattn_WK, L1_xattn_bK, L1_xattn_WV, L1_xattn_bV, L1_xattn_Wl, L1_xattn_bl, L1_ffn_W_fc, L1_ffn_W_proj):
    import jax
    import jax.numpy as jnp

    def _L0_xattn_ref(queries, keys, values, boxes, Wq, bq, Wk, bk, Wv, bv, Wo, bo, Wg, bg):
        import jax, jax.numpy as jnp
        import numpy as np
        D_MODEL = 256
        H = 16
        D_K = 64
        D_V = 64
        D_G = D_MODEL // H
        WAVE_LEN = 1000.0
        B = 8
        N = 128

        def box_relational_embedding(boxes, dim_g=D_G):
            x_min, y_min, x_max, y_max = jnp.split(boxes, 4, axis=-1)
            cx = (x_min + x_max) * 0.5
            cy = (y_min + y_max) * 0.5
            w = x_max - x_min + 1.0
            h = y_max - y_min + 1.0
            delta_x = jnp.log(jnp.clip(jnp.abs((cx - jnp.swapaxes(cx, 1, 2)) / w), 0.001, None))
            delta_y = jnp.log(jnp.clip(jnp.abs((cy - jnp.swapaxes(cy, 1, 2)) / h), 0.001, None))
            delta_w = jnp.log(w / jnp.swapaxes(w, 1, 2))
            delta_h = jnp.log(h / jnp.swapaxes(h, 1, 2))
            pos = jnp.stack([delta_x, delta_y, delta_w, delta_h], axis=-1)
            n_freq = dim_g // 8
            feat_range = jnp.arange(n_freq, dtype=jnp.float32)
            dim_mat = 1.0 / WAVE_LEN ** (feat_range / n_freq)
            mul = (100.0 * pos)[..., None] * dim_mat
            b, n = (pos.shape[0], pos.shape[1])
            mul = mul.reshape(b, n, n, 4 * n_freq)
            return jnp.concatenate([jnp.sin(mul), jnp.cos(mul)], axis=-1)
        b, nq, _ = queries.shape
        nk = keys.shape[1]
        emb = box_relational_embedding(boxes)
        g = jax.nn.relu(jnp.einsum('bnmd,hd->bhnm', emb, Wg) + bg[None, :, None, None])
        q = (queries @ Wq.T + bq).reshape(b, nq, H, D_K).transpose(0, 2, 1, 3)
        k = (keys @ Wk.T + bk).reshape(b, nk, H, D_K).transpose(0, 2, 1, 3)
        v = (values @ Wv.T + bv).reshape(b, nk, H, D_V).transpose(0, 2, 1, 3)
        a = jnp.einsum('bhqd,bhkd->bhqk', q, k) / jnp.sqrt(jnp.float32(D_K))
        mn = jax.nn.softmax(jnp.log(jnp.clip(g, 1e-06, None)) + a, axis=-1)
        out = jnp.einsum('bhqk,bhkd->bqhd', mn, v).reshape(b, nq, H * D_V)
        return out @ Wo.T + bo

    def _L0_ffn_ref(x, in_proj_w, in_proj_b, out_proj_w, out_proj_b, ln1_g, ln1_b, ln2_g, ln2_b, wg, w1, b1, w2, b2):
        import jax, jax.numpy as jnp
        import numpy as np
        D = 256
        H = 4
        HD = D // H
        E = 8
        FF = 1024
        CAP_FACTOR = 1.0

        def _ln(x, g, b, eps=1e-05):
            mu = jnp.mean(x, -1, keepdims=True)
            v = jnp.mean((x - mu) ** 2, -1, keepdims=True)
            return (x - mu) * jax.lax.rsqrt(v + eps) * g + b

        def _mha(x, w, b, ow, ob):
            L, N, _ = x.shape
            qkv = x @ w.T + b
            q, k, v = jnp.split(qkv, 3, axis=-1)
            rh = lambda t: t.reshape(L, N, H, HD).transpose(1, 2, 0, 3)
            q, k, v = (rh(q), rh(k), rh(v))
            scores = jnp.einsum('nhld,nhmd->nhlm', q, k) / np.float32(np.sqrt(HD))
            attn = jax.nn.softmax(scores, axis=-1)
            o = jnp.einsum('nhlm,nhmd->nhld', attn, v).transpose(2, 0, 1, 3).reshape(L, N, D)
            return o @ ow.T + ob

        def _moe(x, wg, w1, b1, w2, b2):
            L, N, _ = x.shape
            S = L * N
            cap = int(CAP_FACTOR * S) // E
            xf = x.reshape(S, D)
            gates = jax.nn.softmax(xf @ wg, axis=-1)
            idx = jnp.argmax(gates, axis=-1)
            mask1 = jax.nn.one_hot(idx, E, dtype=x.dtype)
            loc = jnp.sum((jnp.cumsum(mask1, 0) - 1.0) * mask1, -1).astype(jnp.int32)
            keep = loc < cap
            gate_val = jnp.take_along_axis(gates, idx[:, None], -1)[:, 0]
            slot = jnp.where(keep, idx.astype(jnp.int32) * cap + loc, E * cap)
            disp = jnp.zeros((E * cap, D), x.dtype).at[slot].set(xf, mode='drop')
            disp = disp.reshape(E, cap, D)
            h = jnp.einsum('ecd,edf->ecf', disp, w1) + b1[:, None, :]
            y = (jnp.einsum('ecf,efd->ecd', h, w2) + b2[:, None, :]).reshape(E * cap, D)
            out = jnp.where(keep[:, None], gate_val[:, None] * y[jnp.minimum(slot, E * cap - 1)], 0.0)
            return out.reshape(L, N, D)
        y1 = _ln(x + _mha(x, in_proj_w, in_proj_b, out_proj_w, out_proj_b), ln1_g, ln1_b)
        y2 = _ln(y1 + _moe(y1, wg, w1, b1, w2, b2), ln2_g, ln2_b)
        return y2

    def _L1_xattn_ref(Q, K, V, WQ, bQ, WK, bK, WV, bV, Wl, bl):
        import jax, jax.numpy as jnp
        import numpy as np
        D = 256
        H = 8
        B, S = (4, 512)
        q = Q @ WQ.T + bQ
        k = K @ WK.T + bK
        v = V @ WV.T + bV
        scale = 1.0 / np.sqrt(D).astype(np.float32)
        scores = jnp.einsum('bqd,bkd->bqk', q, k) * scale
        attn = jax.nn.softmax(scores, axis=-1)
        Z = jnp.einsum('bqk,bkd->bqd', attn, v)
        Zcat = jnp.tile(Z, (1, 1, H))
        return Zcat @ Wl.T + bl

    def _L1_ffn_ref(x, W_fc, W_proj):
        import jax, jax.numpy as jnp
        import numpy as np
        import math
        BETA = 0.9
        THRESHOLD = 1.0
        NUM_STEPS = 5
        ALPHA = 2.0

        @jax.custom_vjp
        def spike_fn(u):
            return (u > 0).astype(u.dtype)

        def _spike_fwd(u):
            return (spike_fn(u), u)

        def _spike_bwd(u, g):
            s = jnp.pi / 2.0 * ALPHA * u
            return (g * (ALPHA / 2.0) / (1.0 + s * s),)
        spike_fn.defvjp(_spike_fwd, _spike_bwd)
        h = jnp.square(jax.nn.relu(jnp.einsum('bsd,fd->bsf', x, W_fc)))
        y = jnp.einsum('bsf,df->bsd', h, W_proj)

        def step(mem, _):
            reset = jax.lax.stop_gradient(spike_fn(mem - THRESHOLD))
            mem_new = BETA * mem + y - reset * THRESHOLD
            spk = spike_fn(mem_new - THRESHOLD)
            return (mem_new, spk)
        mem0 = jnp.zeros_like(y)
        _, spks = jax.lax.scan(step, mem0, None, length=NUM_STEPS)
        return jnp.sum(spks, axis=0) / NUM_STEPS
    x = x + jnp.tanh(g_xattn[0]) * _L0_xattn_ref(_layernorm(x, axis=-1), ctx_1024, ctx_1024, fside_BxSx4_0, L0_xattn_Wq, L0_xattn_bq, L0_xattn_Wk, L0_xattn_bk, L0_xattn_Wv, L0_xattn_bv, L0_xattn_Wo, L0_xattn_bo, L0_xattn_Wg, L0_xattn_bg)
    x = x + jnp.tanh(g_ffn[0]) * _L0_ffn_ref(_layernorm(x, axis=-1), L0_ffn_in_proj_w, L0_ffn_in_proj_b, L0_ffn_out_proj_w, L0_ffn_out_proj_b, L0_ffn_ln1_g, L0_ffn_ln1_b, L0_ffn_ln2_g, L0_ffn_ln2_b, L0_ffn_wg, L0_ffn_w1, L0_ffn_b1, L0_ffn_w2, L0_ffn_b2)
    x = x + jnp.tanh(g_xattn[1]) * _L1_xattn_ref(_layernorm(x, axis=-1), ctx_1024, ctx_1024, L1_xattn_WQ, L1_xattn_bQ, L1_xattn_WK, L1_xattn_bK, L1_xattn_WV, L1_xattn_bV, L1_xattn_Wl, L1_xattn_bl)
    x = x + jnp.tanh(g_ffn[1]) * _L1_ffn_ref(_layernorm(x, axis=-1), L1_ffn_W_fc, L1_ffn_W_proj)
    return x

_drawn_inputs = setup_inputs


def setup_inputs(seed=0):
    import zlib

    import numpy as np

    out = dict(_drawn_inputs(seed))
    spreads = {'g_ffn': (-1.0, 0.2),
     'L0_xattn_bq': (0.0, 0.8),
     'L0_xattn_bk': (0.0, 2.0),
     'L0_xattn_bv': (0.0, 0.1),
     'L0_xattn_bo': (0.0, 0.1),
     'L0_xattn_bg': (0.0, 0.1),
     'L0_ffn_in_proj_b': (0.0, 0.1),
     'L0_ffn_out_proj_b': (0.0, 0.1),
     'L0_ffn_ln1_g': (1.0, 0.2),
     'L0_ffn_ln1_b': (0.0, 0.1),
     'L0_ffn_ln2_g': (1.0, 0.2),
     'L0_ffn_ln2_b': (0.0, 0.1),
     'L0_ffn_b1': (0.0, 0.1),
     'L0_ffn_b2': (0.0, 0.1)}
    factors = {'L0_xattn_Wq': 3.558, 'L0_xattn_Wk': 3.549, 'L1_xattn_bQ': 24.286, 'L1_xattn_bK': 64.0}
    for name, (base, spread) in spreads.items():
        noise = np.random.default_rng([zlib.crc32(name.encode()), seed]).standard_normal(out[name].shape)
        drawn = base * np.exp(spread * noise) if base else spread * noise
        out[name] = jnp.asarray(drawn.astype(out[name].dtype))
    for name, factor in factors.items():
        out[name] = (out[name] * factor).astype(out[name].dtype)
    return out
```

```python
import math
from contextlib import ExitStack, contextmanager

import numpy as np

import concourse.bass as bass
from concourse import mybir

F32 = mybir.dt.float32
F16 = mybir.dt.float16
ALU = mybir.AluOpType
ACT = mybir.ActivationFunctionType
AXIS_X = mybir.AxisListType.X

P = 128
B, S, D = 8, 512, 256
C = D // P
T = B * S
H0, DK = 16, 64
PAIRS = H0 // 2
HG = H0 // 4
QB = S // P
NT = S // 32
KT = S // P
HM, DM = 4, 64
E, FF = 8, 1024
CAP = T // E
WAVE = 1000.0
TURN = 6.283185
ROUND = 12582912.0
WSCALE = 64.0
CLIP = 1e-6
EPS = 1e-5
MASKED = -1e30
SEP = 9


class Mark:

    def __init__(self, sem, value):
        self.sem, self.value = sem, value


class Counter:

    def __init__(self, nc, name, table, prime=0):
        self.name, self.sem, self.table = name, nc.alloc_semaphore(name), table
        self.base, self.k, self.frames = prime, 0, []

    def enter(self, loop, i):
        per = self.table["per"].get((loop, self.name), 1)
        self.frames.append((loop, self.base, self.k, per))
        self.base, self.k = (self.base + self.k) + i * per if per else self.base + self.k, 0

    def leave(self, rounds):
        loop, base, k, _ = self.frames.pop()
        per = self.table["new_per"][(loop, self.name)] = self.k
        self.base, self.k = base, k + rounds * per

    def mark(self, ins, name=None, step=1):
        ins.then_inc(self.sem, step)
        self.k += step
        if name is not None:
            self.table["new_names"][(self.name, name)] = self.k
        return Mark(self.sem, self.base + self.k)

    def now(self):
        return Mark(self.sem, self.base + self.k)

    def before(self, name):
        per = self.frames[-1][3]
        return Mark(self.sem, self.base + (self.table["names"].get((self.name, name), 1) - per))


class Engine:

    def __init__(self, nc, name, eng, table, prime):
        self.e = eng
        self.count = Counter(nc, name, table, prime)
        if prime:
            eng.sem_inc(self.count.sem, prime)

    def wait(self, *marks):
        for m in marks:
            if m is not None:
                self.e.wait_ge(m.sem, m.value)

    def __call__(self, ins_of, *marks, name=None):
        self.wait(*marks)
        return self.count.mark(ins_of(self.e), name)


def build(nc, table, io):
    o = io.__getitem__
    PRIME = 1200
    pe = Engine(nc, "pe", nc.tensor, table, PRIME)
    act = Engine(nc, "act", nc.scalar, table, PRIME)
    dve = Engine(nc, "dve", nc.vector, table, PRIME)
    pool = Engine(nc, "pool", nc.gpsimd, table, PRIME)
    dmas = {}

    def dma_counter(name):
        if name not in dmas:
            dmas[name] = Counter(nc, "dma_" + name, table)
            assert not loops, name
        return dmas[name]

    loops = []

    @contextmanager
    def loop(name, n):
        with nc.Fori(0, n) as i:
            loops.append(name)
            every = [pe.count, act.count, dve.count, pool.count, *dmas.values()]
            for c in every:
                c.enter(name, i)
            yield i
            for c in every:
                c.leave(n)
            loops.pop()

    def load(name, dst, src, *marks, eng=None):
        q = eng or nc.sync
        for m in marks:
            if m is not None:
                q.wait_ge(m.sem, m.value)
        return dma_counter(name).mark(q.dma_start(dst, src), step=16)

    for name in ("const", "wx", "x", "ctx", "x1out", "z", "w1", "w2", "b1", "wb", "x1in", "ctx1", "out"):
        dma_counter(name)

    def barrier():
        nc.all_engine_barrier()

    def sb(ctx, name, shape, dt=F32):
        return ctx.enter_context(nc.sbuf_tensor(name, shape, dt))

    x1_dram = nc.dram_tensor("x1_scratch", (B, C, P, S), F32, kind="Internal").ap()

    with ExitStack() as top:
        bank = [top.enter_context(nc.psum_tensor(f"bank{i}", [P, 512], F32)) for i in range(8)]

        ident = sb(top, "ident", [P, P])
        ones_mean = sb(top, "ones_mean", [P, P])
        gates = sb(top, "gates", [P, 4])
        tanh_g = sb(top, "tanh_g", [P, 4])
        cols = sb(top, "cols", [P, len(COLS)])
        eps_col = sb(top, "eps_col", [P, 1])

        def col(name, c=0):
            k = COLS.index((name, c))
            return cols[:, k:k + 1]

        load("const", ident[:, :], o("ident"))
        load("const", cols[:, :], o("cols"))
        c_in = load("const", gates[:, :], o("gates").partition_broadcast(P))
        ones_m = dve(lambda e: e.memset(ones_mean[:, :], 1.0 / D))
        dve(lambda e: e.memset(eps_col[:, :], EPS))
        act(lambda e: e.activation(tanh_g[:, :], gates[:, :], ACT.Tanh), c_in)
        barrier()
        TX0, TX1, TF0, TF1 = (tanh_g[:, i:i + 1] for i in range(4))

        def matmul(out, pairs, *marks, name=None):
            pe.wait(*marks)
            for n, (lhsT, rhs) in enumerate(pairs):
                last = nc.tensor.matmul(out, lhsT, rhs, start=(n == 0), stop=(n == len(pairs) - 1))
            return pe.count.mark(last, name)

        def layernorm(src, dst, sq, std, mean_ps, var_ps, ready, free, scale=None, shift=None,
                      shaped=lambda a: a):
            m_mean = matmul(mean_ps, [(ones_mean[:, :], src(c)) for c in range(C)], *ready, *free)
            m_sq = []
            for c in range(C):
                m_c = dve(lambda e: e.tensor_tensor(shaped(dst(c)), src(c), shaped(mean_ps), ALU.subtract), m_mean)
                m_sq.append(act(lambda e: e.activation(sq[:, c, :], dst(c), ACT.Square), m_c))
            m_var = matmul(var_ps, [(ones_mean[:, :], sq[:, c, :]) for c in range(C)], m_sq[-1])
            m_std = act(lambda e: e.activation(std[:, :], var_ps, ACT.Sqrt, bias=eps_col[:, 0:1]), m_var)
            m_r = dve(lambda e: e.reciprocal(std[:, :], std[:, :]), m_std)
            out = []
            for c in range(C):
                m = dve(lambda e: e.tensor_tensor(dst(c), dst(c), std[:, :], ALU.mult), m_r)
                out.append(m)
            if scale is not None:
                out = [dve(lambda e: e.tensor_scalar(dst(c), dst(c), scale(c), shift(c), ALU.mult, ALU.add),
                           out[c]) for c in range(C)]
            return out

        with ExitStack() as ctx:
            wq = sb(ctx, "wq", [P, C, H0 * DK])
            wk = sb(ctx, "wk", [P, C, H0 * DK])
            wv = sb(ctx, "wv", [P, C, H0 * DK])
            wo = sb(ctx, "wo", [P, PAIRS, D])
            rel_w = sb(ctx, "rel_w", [P, 2, H0])
            sep_w = sb(ctx, "sep_w", [P, 2, HG])
            fold = sb(ctx, "fold", [P, P])
            kron = sb(ctx, "kron", [P, 2, 2, H0, 32], F16)
            kron_w = sb(ctx, "kron_w", [P, 32])
            sel = sb(ctx, "sel", [4, 2, P])
            box_lo = sb(ctx, "box_lo", [P, B * NT])
            box_hi = sb(ctx, "box_hi", [P, B * NT])
            centre = sb(ctx, "centre", [P, B * NT])
            inv_size = sb(ctx, "inv_size", [P, B * NT])
            cen_b = sb(ctx, "cen_b", [P, 2, NT])
            xin = sb(ctx, "xin", [P, C, S])
            cin = sb(ctx, "cin", [P, C, S])
            box = sb(ctx, "box", [4, S])
            kT = sb(ctx, "kT", [P, PAIRS, S])
            qT = sb(ctx, "qT", [P, PAIRS, S])
            vv = sb(ctx, "vv", [P, KT, H0 * DK])
            feat = sb(ctx, "feat", [P, NT, 2, 2, S], F16)
            feat32 = feat[:, :, :, :, :].rearrange("p j f x s -> p j f (x s)").bitcast(F32)
            sepA = sb(ctx, "sepA", [P, HG, S], F16)
            sepB = sb(ctx, "sepB", [P, S], F16)
            qbd = sb(ctx, "qbd", [P, 2, 2, QB, DK])
            abd = sb(ctx, "abd", [P, 2, QB, P], F16)
            ptT = sb(ctx, "ptT", [P, 2, KT, 4, P])
            eb = sb(ctx, "eb", [P, 2, S])
            pb = sb(ctx, "pb", [P, 2, S])
            small = sb(ctx, "small", [P, 2, 4])
            xn = ptT[:, 0, 0:2, :, :].rearrange("p a h q -> p a (h q)")
            lnsq = ptT[:, 0, 2:4, :, :].rearrange("p a h q -> p a (h q)")
            fb = [ptT[:, 1, i, :, :].rearrange("p h q -> p (h q)") for i in range(4)]
            std = eb[:, 0, :]
            rb = eb[:, 1, :]
            sa, sbb = pb[:, 0, :], pb[:, 1, :]

            for dst, src in ((wq, "wqT"), (wk, "wkT"), (wv, "wvT"), (wo, "woT")):
                load("wx", dst[:, :, :], o(src).rearrange("(c p) n -> p c n", p=P))
            load("wx", rel_w[:, :, :], o("rel_w"))
            load("wx", sep_w[:, :, :], o("sep_w"))
            load("wx", fold[:, :], o("fold"))
            load("wx", sel[:, :, :], o("sel"))
            load("wx", box_lo[:, :], o("box_lo"))
            wx = load("wx", box_hi[:, :], o("box_hi"))

            m = dve(lambda e: e.tensor_tensor(centre[:, :], box_lo[:, :], box_hi[:, :], ALU.add), wx)
            dve(lambda e: e.tensor_scalar(centre[:, :], centre[:, :], 0.5, None, ALU.mult), m)
            m = dve(lambda e: e.tensor_tensor(inv_size[:, :], box_hi[:, :], box_lo[:, :], ALU.subtract))
            m = dve(lambda e: e.tensor_scalar(inv_size[:, :], inv_size[:, :], 1.0, None, ALU.add), m)
            dve(lambda e: e.reciprocal(inv_size[:, :], inv_size[:, :]), m)
            dve(lambda e: e.tensor_scalar(sep_w[:, :, :], sep_w[:, :, :], WSCALE, None, ALU.mult), wx)
            m_rw = dve(lambda e: e.tensor_scalar(rel_w[:, :, :], rel_w[:, :, :], WSCALE, None, ALU.mult), wx)
            for f in range(2):
                for h in range(H0):
                    m = dve(lambda e: e.tensor_scalar(kron_w[:, :], fold[:, 0:32], rel_w[:, f, h:h + 1], None,
                                                      ALU.mult), m_rw, dve.count.now())
                    m = dve(lambda e: e.tensor_copy(kron[:, f, 0, h, :], kron_w[:, :]), m)
                    dve(lambda e: e.tensor_tensor(kron[:, f, 1, h, :], kron_w[:, :], kron[:, f, 0, h, :],
                                                  ALU.subtract), m)
            pool(lambda e: e.memset(qbd[:, :, :, :, :], 0.0))
            pool(lambda e: e.memset(abd[:, :, :, :], 0.0))
            barrier()

            with loop("xattn0", B) as b:
                barrier()
                load("x", xin[:, :, :], o("xT")[bass.ds(b, 1)].rearrange("o c p s -> p (o c) s"))
                x_in = load("x", box[:, :], o("boxT")[bass.ds(b, 1)].rearrange("o k s -> (o k) s"))
                c_in = load("ctx", cin[:, :, :], o("ctxT")[bass.ds(b, 1)].rearrange("o c p s -> p (o c) s"))

                bank_free = [None] * 8

                def project(dst_of, w, rhs, ready, n, banks, finish):
                    for i in range(n):
                        k = banks[i % len(banks)]
                        m = matmul(bank[k][:, :], [(w[:, c, i * P:(i + 1) * P], rhs[:, c, :]) for c in range(C)],
                                   *ready, bank_free[k])
                        bank_free[k] = finish(i, bank[k][:, :], m)

                project(None, wk, cin, [c_in], PAIRS, [2, 3], lambda i, ps, m: act(
                    lambda e: e.activation(kT[:, i, :], ps, ACT.Identity, bias=col("bk", i)), m))

                for kt in range(KT):
                    for n in range(2):
                        k = 4 + (2 * kt + n) % 2
                        m = matmul(bank[k][:, :], [(cin[:, c, kt * P:(kt + 1) * P], wv[:, c, n * 512:(n + 1) * 512])
                                                   for c in range(C)], bank_free[k])
                        bank_free[k] = act(lambda e: e.activation(vv[:, kt, n * 512:(n + 1) * 512], bank[k][:, :],
                                                                  ACT.Copy), m)

                m_xn = layernorm(lambda c: xin[:, c, :], lambda c: xn[:, c, :], lnsq, std,
                                 bank[0][:, :], bank[1][:, :], [x_in], [])
                project(None, wq, xn, m_xn, PAIRS, [2, 3], lambda i, ps, m: dve(
                    lambda e: e.tensor_scalar(qT[:, i, :], ps, col("bq", i), DK ** -0.5, ALU.add, ALU.mult), m))
                m_q = dve.count.now()

                m = matmul(bank[6][:, :], [(sel[:, 0, :], box[:, :])])
                m_rb = dve(lambda e: e.tensor_scalar(rb, bank[6][:, :], 0.5, None, ALU.mult), m)
                m = matmul(bank[7][:, :], [(sel[:, 1, :], box[:, :])])
                m = act(lambda e: e.activation(fb[0], bank[7][:, :], ACT.Ln, bias=1.0), m, m_q)
                m_l = dve(lambda e: e.tensor_scalar(fb[0], fb[0], col("sep_freq"), None, ALU.mult), m)
                sep_m = []
                for phase, dst in ((col("phase1"), sa), (col("phase2"), sbb)):
                    m = dve(lambda e: e.tensor_scalar(fb[1], fb[0], phase, None, ALU.add), m_l, dve.count.now())
                    m = dve(lambda e: e.tensor_scalar(fb[2], fb[1], ROUND, -ROUND, ALU.add, ALU.add), m)
                    m = dve(lambda e: e.tensor_tensor(fb[3], fb[1], fb[2], ALU.subtract), m)
                    sep_m.append(act(lambda e: e.activation(dst, fb[3], ACT.Sin, scale=TURN), m))
                    dve.wait(sep_m[-1])
                m = dve(lambda e: e.tensor_copy(sepB[:, :], sa), sep_m[0])
                m = dve(lambda e: e.tensor_tensor(fb[1], sa, sepB[:, :], ALU.subtract), m)
                m = dve(lambda e: e.tensor_scalar(fb[1], fb[1], col("b_low"), None, ALU.mult), m)
                m = dve(lambda e: e.scalar_tensor_tensor(sepB[:, :], sepB[:, :], col("b_high"), fb[1],
                                                         ALU.mult, ALU.add), m)
                for g in range(HG):
                    m = dve(lambda e: e.tensor_scalar(fb[1], sa, sep_w[:, 0, g:g + 1], None, ALU.mult),
                            dve.count.now())
                    m = dve(lambda e: e.scalar_tensor_tensor(fb[1], sbb, sep_w[:, 1, g:g + 1], fb[1],
                                                             ALU.mult, ALU.add), m)
                    m = dve(lambda e: e.tensor_copy(sepA[:, g, :], fb[1]), m)
                    m = dve(lambda e: e.tensor_tensor(fb[2], fb[1], sepA[:, g, :], ALU.subtract), m)
                    m = dve(lambda e: e.tensor_scalar(fb[2], fb[2], col("a_low"), None, ALU.mult), m)
                    m = dve(lambda e: e.scalar_tensor_tensor(sepA[:, g, :], sepA[:, g, :], col("a_high"), fb[2],
                                                             ALU.mult, ALU.add), m)
                m_sep = m

                m = dve(lambda e: e.tensor_scalar(cen_b[:, 0, :], centre[:, bass.ds(b * NT, NT)], -1.0, None,
                                                  ALU.mult))
                m_c = dve(lambda e: e.tensor_copy(cen_b[:, 1, :], inv_size[:, bass.ds(b * NT, NT)]))
                act.wait(m_rb, m_c)
                for j0 in range(0, NT, 4):
                    quad = slice(j0, j0 + 4)
                    for j in range(j0, j0 + 4):
                        m = act(lambda e: e.activation(feat32[:, j, 0, :], rb, ACT.Abs, bias=cen_b[:, 0, j:j + 1]))
                        m = dve(lambda e: e.tensor_scalar(feat32[:, j, 0, :], feat32[:, j, 0, :],
                                                          cen_b[:, 1, j:j + 1], 1e-3, ALU.mult, ALU.max), m)
                    m = act(lambda e: e.activation(feat32[:, quad, 0, :], feat32[:, quad, 0, :], ACT.Ln), m)
                    m = dve(lambda e: e.tensor_scalar(feat32[:, quad, 0, :], feat32[:, quad, 0, :],
                                                      col("pix_freq"), None, ALU.mult), m)
                    m = dve(lambda e: e.tensor_scalar(feat32[:, quad, 1, :], feat32[:, quad, 0, :],
                                                      ROUND, -ROUND, ALU.add, ALU.add), m)
                    m_t = dve(lambda e: e.tensor_tensor(feat32[:, quad, 0, :], feat32[:, quad, 0, :],
                                                        feat32[:, quad, 1, :], ALU.subtract), m)
                    m_a = act(lambda e: e.activation(feat32[:, quad, 1, :], feat32[:, quad, 0, :], ACT.Abs), m_t)
                act.wait(m_a)
                m_low = {}
                for n in range(2 * NT):
                    j, f, tmp = n // 2, n % 2, fb[n % 4]
                    if f == 0:
                        m = act(lambda e: e.activation(tmp, feat32[:, j, 0, :], ACT.Sin, scale=TURN),
                                dve.count.now() if n < 4 else m_low[n - 4])
                    else:
                        m = act(lambda e: e.activation(tmp, feat32[:, j, 1, :], ACT.Sin, scale=-TURN,
                                                       bias=col("quarter")), m_low.get(n - 4))
                    m = dve(lambda e: e.tensor_copy(feat[:, j, f, 0, :], tmp), m)
                    m_low[n] = pool(lambda e: e.tensor_tensor(feat[:, j, f, 1, :], tmp, feat[:, j, f, 0, :],
                                                              ALU.subtract), m)

                def block_diagonals(g, q, *marks):
                    s = g % 2
                    act.wait(*marks)
                    for h in range(2):
                        rows = slice(64 * h, 64 * h + 64)
                        src = qT[rows, 2 * g:2 * g + 2, bass.ds(q * P, P)].rearrange("p a (j i) -> p a j i", i=32)
                        act(lambda e: e.activation(qbd[rows, s, :, :, 32 * h:32 * h + 32], src, ACT.Copy))
                    for h in range(4):
                        rows = slice(32 * h, 32 * h + 32)
                        src = sepA[rows, g, bass.ds(q * P, P)].rearrange("p (j i) -> p j i", i=32)
                        m = act(lambda e: e.activation(abd[rows, s, :, 32 * h:32 * h + 32], src, ACT.Copy))
                    return m

                m_bd_first = block_diagonals(0, 0, m_q, m_sep)
                barrier()

                with loop("qblock", QB) as q:
                    NTILE = HG * QB
                    Sb, Gb, Tb, Ob = bank[0:2], bank[2:4], bank[4:6], bank[6:8]
                    m_S, m_G, m_TR, m_exp, m_P, m_ev, m_stt = ({} for _ in range(7))
                    m_bd = {0: act.count.before("bd0")}
                    m_pv = {}
                    m_ov = {}

                    def finish_tile(t):
                        s = t % 2
                        free = m_TR[t - 2] if t >= 2 else pe.count.before(f"tr{t + 14}")
                        m_stt[t] = dve(lambda e: e.scalar_tensor_tensor(
                            pb[:, s, :], Gb[s][:, :], CLIP * WSCALE, eb[:, s, :], ALU.max, ALU.mult,
                            accum_out=small[:, s, 0:1]), m_G[t], m_exp[t], free, name=f"stt{t}")
                        m = dve(lambda e: e.reciprocal(small[:, s, 1:2], small[:, s, 0:1]), m_stt[t])
                        m_P[t] = dve(lambda e: e.tensor_scalar(pb[:, s, :], pb[:, s, :], small[:, s, 1:2], None,
                                                               ALU.mult), m, name=f"P{t}")

                    def transpose_tile(t):
                        s, g, j = t % 2, t // QB, t % QB
                        free = m_ev[t - 2] if t >= 2 else act.count.before(f"ev{t + 14}")
                        pe.wait(m_P[t], free)
                        for kt in range(KT):
                            last = nc.tensor.transpose(Tb[s][:, kt * P:(kt + 1) * P],
                                                       pb[:, s, kt * P:(kt + 1) * P], ident[:, :])
                        m_TR[t] = pe.count.mark(last, f"tr{t}")
                        free = m_pv.get(g - 2) or pe.count.before(f"pv{g + 2}")
                        m_ev[t] = act(lambda e: e.activation(
                            ptT[:, g % 2, :, :, 32 * j:32 * j + 32],
                            Tb[s][:, :].rearrange("p (k h i) -> p k h i", k=KT, h=4), ACT.Copy),
                            m_TR[t], free, name=f"ev{t}")

                    def values(g):
                        out = Ob[g % 2]
                        pe.wait(m_ev[QB * g + QB - 1], m_ov.get(g - 2) or dve.count.before(f"ov{g + 2}"))
                        for a in range(2):
                            for kt in range(KT):
                                for h in range(2):
                                    hh = 2 * a + h
                                    last = nc.tensor.matmul(
                                        out[64 * h:64 * h + 64, a * P:(a + 1) * P],
                                        vv[:, kt, (4 * g + hh) * DK:(4 * g + hh + 1) * DK],
                                        ptT[:, g % 2, kt, hh, :], start=(kt == 0), stop=(kt == KT - 1))
                        m_pv[g] = pe.count.mark(last, f"pv{g}")
                        for a in range(2):
                            m_ov[g] = dve(lambda e: e.tensor_scalar(
                                qT[:, 2 * g + a, bass.ds(q * P, P)], out[:, a * P:(a + 1) * P],
                                col("bv", 2 * g + a), None, ALU.add), m_pv[g], name=f"ov{g}" if a else None)

                    for t in range(NTILE):
                        s, g, j = t % 2, t // QB, t % QB
                        if j == 0:
                            pe.wait(m_bd[g])
                        pe.wait(m_exp[t - 2] if t >= 2 else act.count.before(f"exp{t + 14}"))
                        for a in range(2):
                            last = nc.tensor.matmul(Sb[s][64 * a:64 * a + 64, :], qbd[:, g % 2, a, j, :],
                                                    kT[:, 2 * g + a, :], start=True, stop=True)
                        m_S[t] = pe.count.mark(last, f"S{t}")
                        grp = q * QB + j
                        pe.wait(m_stt[t - 2] if t >= 2 else dve.count.before(f"stt{t + 14}"))
                        nc.tensor.matmul(Gb[s][:, :], abd[:, g % 2, j, :], sepB[:, :], start=True, stop=False)
                        for f in range(2):
                            for w, x in ((0, 0), (0, 1), (1, 0)):
                                last = nc.tensor.matmul(
                                    Gb[s][:, :], kron[:, f, w, 4 * g:4 * g + 4, :].rearrange("p h i -> p (h i)"),
                                    feat[:, bass.ds(grp, 1), f, x, :].rearrange("p o s -> p (o s)"),
                                    start=False, stop=(f == 1 and w == 1))
                        m_G[t] = pe.count.mark(last, f"G{t}")
                        if j == 1:
                            n = g + 1
                            if n < HG:
                                free = m_G[QB * n - 5] if n >= 2 else pe.count.before("G15")
                                m_bd[n] = block_diagonals(n, q, free)
                        if t == NTILE - 1 - 2:
                            block_diagonals_next = m_G[QB * 3 - 1]
                            qn = (q + 1) % QB
                            block_diagonals(0, qn, block_diagonals_next)
                            table["new_names"][("act", "bd0")] = act.count.k

                        if t >= 1:
                            finish_tile(t - 1)
                        free = m_exp[t - 2] if t >= 2 else act.count.before(f"exp{t + 14}")
                        m = dve(lambda e: e.tensor_reduce(small[:, s, 2:3], Sb[s][:, :], AXIS_X, ALU.max),
                                m_S[t], free)
                        m = dve(lambda e: e.tensor_scalar(small[:, s, 3:4], small[:, s, 2:3], -1.0, None,
                                                          ALU.mult), m)
                        free = m_stt[t - 2] if t >= 2 else dve.count.before(f"stt{t + 14}")
                        m_exp[t] = act(lambda e: e.activation(eb[:, s, :], Sb[s][:, :], ACT.Exp,
                                                              bias=small[:, s, 3:4]), m, free, name=f"exp{t}")
                        if t >= 1:
                            transpose_tile(t - 1)
                        if t >= 2 and (t - 2) % QB == QB - 1:
                            values((t - 2) // QB)
                    finish_tile(NTILE - 1)
                    transpose_tile(NTILE - 1)
                    values(HG - 1)

                barrier()
                for c in range(C):
                    m = matmul(bank[c][:, :], [(wo[:, i, c * P:(c + 1) * P], qT[:, i, :]) for i in range(PAIRS)])
                    m = dve(lambda e: e.tensor_scalar(xn[:, c, :], bank[c][:, :], col("bo", c), TX0,
                                                      ALU.add, ALU.mult), m)
                    m = dve(lambda e: e.tensor_tensor(xin[:, c, :], xin[:, c, :], xn[:, c, :], ALU.add), m)
                x1_out = load("x1out", x1_dram[bass.ds(b, 1)].rearrange("o c p s -> p (o c) s"), xin[:, :, :], m)
                nc.sync.wait_ge(x1_out.sem, x1_out.value)
                barrier()

        with ExitStack() as outer:
            y1T = sb(outer, "y1T", [P, C, T])
            logits = sb(outer, "logits", [P, T // P, E])
            coef = sb(outer, "coef", [P, T // P, E])
            w12 = sb(outer, "w12", [P, E, C, D])
            b12 = sb(outer, "b12", [E, D])
            with ExitStack() as ctx:
                w_in = sb(ctx, "w_in", [P, C, 3 * D])
                w_out = sb(ctx, "w_out", [P, C, D])
                mask = sb(ctx, "mask", [P, P])
                zin = sb(ctx, "zin", [P, C, B, 64])
                z = sb(ctx, "z", [P, C, 512])
                sq = sb(ctx, "sq", [P, C, 512])
                std = sb(ctx, "stdb", [P, 512])
                qk = sb(ctx, "qk", [P, 4, 4, P])
                vt = sb(ctx, "vt", [P, 4, D])
                sm = sb(ctx, "sm", [P, 2, HM, P])
                pt = sb(ctx, "pt", [P, 2, HM, P])
                stat = sb(ctx, "stat", [P, 2, 3, HM])
                oT = sb(ctx, "oT", [P, C, 512])
                yb = sb(ctx, "yb", [P, C, 512])
                w1e = sb(ctx, "w1e", [P, FF // P, D])
                w2e = sb(ctx, "w2e", [P, FF // P, D])
                b1e = sb(ctx, "b1e", [P, FF // P, E])
                load("wb", w_in[:, :, :], o("in_wT").rearrange("(c p) n -> p c n", p=P))
                load("wb", w_out[:, :, :], o("out_wT").rearrange("(c p) n -> p c n", p=P))
                load("wb", mask[:, :], o("mask"))
                load("wb", b12[:, :], o("b2"))
                barrier()

                with loop("experts", E) as x:
                    barrier()
                    a = load("w1", w1e[:, :, :], o("w1T")[bass.ds(x, 1)].rearrange("o (k p) d -> p (o k) d", p=P))
                    c_ = load("w2", w2e[:, :, :], o("w2")[bass.ds(x, 1)].rearrange("o (k p) d -> p (o k) d", p=P))
                    d_ = load("b1", b1e[:, :, :], o("b1x")[bass.ds(x, 1)].rearrange("o p k e -> p (o k) e"))
                    for c in range(C):
                        m = matmul(bank[c][:, 0:D], [(w1e[:, k, c * P:(c + 1) * P], w2e[:, k, :])
                                                     for k in range(FF // P)], a, c_)
                        act(lambda e: e.activation(w12[:, bass.ds(x, 1), c, :].rearrange("p o d -> p (o d)"),
                                                   bank[c][:, 0:D], ACT.Copy), m)
                    m = matmul(bank[2][0:E, 0:D], [(b1e[:, k, :], w2e[:, k, :]) for k in range(FF // P)], d_)
                    dve(lambda e: e.tensor_tensor(b12[:, :], b12[:, :], bank[2][0:E, 0:D], ALU.add), m,
                        dmas["wb"].now())
                barrier()

                with loop("mha", S // 64) as sblk:
                    barrier()
                    for c in range(C):
                        z_in = load("z", zin[:, c, :, :],
                                    x1_dram[:, c, :, bass.ds(sblk * 64, 64)].rearrange("b p s -> p b s"))
                    m_z = layernorm(lambda c: zin[:, c, :, :].rearrange("p b (t s) -> p t b s", t=4),
                                    lambda c: z[:, c, :], sq, std, bank[0][:, :], bank[1][:, :], [z_in], [],
                                    shaped=lambda a: a.rearrange("p (t b s) -> p t b s", t=4, b=B))
                    free = {}
                    for i in range(4):
                        k = 2 + i % 2
                        m = matmul(bank[k][:, :], [(w_in[:, c, i * P:(i + 1) * P], z[:, c, :]) for c in range(C)],
                                   *m_z, free.get(k))
                        free[k] = dve(lambda e: e.tensor_scalar(
                            qk[:, i, :, :].rearrange("p t n -> p (t n)"), bank[k][:, :], col("b_in", i),
                            DM ** -0.5 if i < 2 else 1.0, ALU.add, ALU.mult), m)
                    for t in range(4):
                        k = 4 + t % 2
                        m = matmul(bank[k][:, 0:D], [(z[:, c, t * P:(t + 1) * P], w_in[:, c, 2 * D:3 * D]) for c in range(C)],
                                   free.get(k))
                        free[k] = act(lambda e: e.activation(vt[:, t, :], bank[k][:, 0:D], ACT.Copy), m)
                    m_q = dve.count.now()
                    m_exp, m_pt, m_tr, m_pv, m_ov, m_sub = {}, {}, {}, {}, {}, {}
                    for t in range(4):
                        s = t % 2
                        pe.wait(m_q, m_sub.get(t - 2), free.get(2 + s), free.get(4 + s))
                        for h in range(HM):
                            rows = slice(64 * (h % 2), 64 * (h % 2) + 64)
                            last = nc.tensor.matmul(bank[s + 4 * (h % 2)][:, (h // 2) * P:(h // 2 + 1) * P],
                                                    qk[rows, h // 2, t, :], qk[rows, 2 + h // 2, t, :],
                                                    start=True, stop=True)
                        m = pe.count.mark(last)
                        for h in range(2):
                            m_sub[t] = dve(lambda e: e.tensor_tensor(
                                sm[:, s, h:HM:2, :],
                                bank[s + 4 * h][:, 0:2 * P].rearrange("p (h k) -> p h k", h=2),
                                mask[:, :].unsqueeze(1).to_broadcast([P, 2, P]), ALU.add), m,
                                m_tr.get(t - 2))
                        m = dve(lambda e: e.tensor_reduce(stat[:, s, 0, :], sm[:, s, :, :], AXIS_X, ALU.max),
                                m_sub[t])
                        m = dve(lambda e: e.tensor_scalar(stat[:, s, 0, :], stat[:, s, 0, :], -1.0, None,
                                                          ALU.mult), m)
                        for h in range(HM):
                            m_e = act(lambda e: e.activation(sm[:, s, h, :], sm[:, s, h, :], ACT.Exp,
                                                             bias=stat[:, s, 0, h:h + 1],
                                                             accum_out=stat[:, s, 1, h:h + 1]), m)
                        m = dve(lambda e: e.reciprocal(stat[:, s, 2, :], stat[:, s, 1, :]), m_e)
                        for h in range(HM):
                            m_p = dve(lambda e: e.tensor_scalar(sm[:, s, h, :], sm[:, s, h, :],
                                                                stat[:, s, 2, h:h + 1], None, ALU.mult), m)
                        pe.wait(m_p, m_pt.get(t - 2))
                        for h in range(HM):
                            last = nc.tensor.transpose(bank[2 + s][:, h * P:(h + 1) * P], sm[:, s, h, :],
                                                       ident[:, :])
                        m_tr[t] = pe.count.mark(last)
                        m_pt[t] = act(lambda e: e.activation(
                            pt[:, s, :, :], bank[2 + s][:, :].rearrange("p (h k) -> p h k", h=HM), ACT.Copy),
                            m_tr[t], m_pv.get(t - 2))
                        pe.wait(m_pt[t], m_ov.get(t - 2))
                        for h in range(HM):
                            last = nc.tensor.matmul(
                                bank[6 + s][64 * (h % 2):64 * (h % 2) + 64, (h // 2) * P:(h // 2 + 1) * P],
                                vt[:, t, h * DM:(h + 1) * DM], pt[:, s, h, :], start=True, stop=True)
                        m_pv[t] = pe.count.mark(last)
                        for c in range(C):
                            m_ov[t] = dve(lambda e: e.tensor_scalar(
                                oT[:, c, t * P:(t + 1) * P], bank[6 + s][:, c * P:(c + 1) * P],
                                col("b_in", 4 + c), None, ALU.add), m_pv[t])
                    for c in range(C):
                        m = matmul(bank[4 + c][:, :], [(w_out[:, i, c * P:(c + 1) * P], oT[:, i, :])
                                                       for i in range(C)], m_ov[3])
                        m_r = dve(lambda e: e.scalar_tensor_tensor(z[:, c, :], bank[4 + c][:, :], col("b_out", c),
                                                                   z[:, c, :], ALU.add, ALU.add), m)
                    layernorm(lambda c: z[:, c, :], lambda c: yb[:, c, :], sq, std, bank[0][:, :],
                              bank[1][:, :], [m_r], [], lambda c: col("ln1_g", c), lambda c: col("ln1_b", c))
                    for c in range(C):
                        y_v = y1T[:, c, :].rearrange("p (b s) -> p b s", b=B)[:, :, bass.ds(sblk * 64, 64)]
                        dve(lambda e: e.tensor_copy(y_v.rearrange("p b (t s) -> p t b s", t=4),
                                                    yb[:, c, :].rearrange("p (t b s) -> p t b s", t=4, b=B)),
                            dve.count.now())
                barrier()

            with ExitStack() as ctx:
                wg = sb(ctx, "wg", [P, C, E])
                tri = sb(ctx, "tri", [P, P])
                ones = sb(ctx, "ones", [P, P])
                rank = sb(ctx, "rank", [P, E])
                ys = sb(ctx, "ys", [P, C, S])
                NTT = T // P
                top1 = sb(ctx, "top1", [P, NTT, 1])
                hot = sb(ctx, "hot", [P, NTT, E])
                wrk = sb(ctx, "wrk", [P, NTT, E])
                pre = [sb(ctx, "pre0", [P, NTT, E]), sb(ctx, "pre1", [P, NTT, E])]
                load("wb", wg[:, :, :], o("wg").rearrange("(c p) n -> p c n", p=P))
                load("wb", tri[:, :], o("tri"))
                m_w = load("wb", rank[:, :], o("rank"))
                dve(lambda e: e.memset(ones[:, :], 1.0))
                nc.sync.wait_ge(m_w.sem, m_w.value)
                barrier()
                with loop("logits", B) as b:
                    for c in range(C):
                        m = dve(lambda e: e.tensor_copy(ys[:, c, :], y1T[:, c, bass.ds(b * S, S)]),
                                pe.count.before("lg"), name="ys")
                    pe.wait(m, dve.count.before("lgc"))
                    for t in range(KT):
                        for c in range(C):
                            last = nc.tensor.matmul(bank[0][:, t * E:(t + 1) * E], ys[:, c, t * P:(t + 1) * P],
                                                    wg[:, c, :], start=(c == 0), stop=(c == C - 1))
                    m = pe.count.mark(last, "lg")
                    dve(lambda e: e.tensor_copy(
                        logits[:, bass.ds(b * KT, KT), :],
                        bank[0][:, 0:KT * E].rearrange("p (t e) -> p t e", t=KT)), m, name="lgc")
                barrier()

                def chain(ins_of):
                    return dve(ins_of, dve.count.now())

                full = [P, NTT, E]
                chain(lambda e: e.tensor_reduce(top1[:, :, 0], logits[:, :, :], AXIS_X, ALU.max))
                chain(lambda e: e.tensor_tensor(wrk[:, :, :], logits[:, :, :], top1[:, :, :].to_broadcast(full),
                                                ALU.subtract))
                chain(lambda e: e.tensor_scalar(hot[:, :, :], wrk[:, :, :], 0.0, None, ALU.is_equal))
                chain(lambda e: e.tensor_tensor(hot[:, :, :], hot[:, :, :],
                                                rank[:, :].unsqueeze(1).to_broadcast(full), ALU.mult))
                chain(lambda e: e.tensor_reduce(top1[:, :, 0], hot[:, :, :], AXIS_X, ALU.max))
                m_hot = chain(lambda e: e.tensor_tensor(hot[:, :, :], hot[:, :, :],
                                                        top1[:, :, :].to_broadcast(full), ALU.is_equal))
                m = act(lambda e: e.activation(wrk[:, :, :], wrk[:, :, :], ACT.Exp), m_hot)
                dve.wait(m)
                chain(lambda e: e.tensor_reduce(top1[:, :, 0], wrk[:, :, :], AXIS_X, ALU.add))
                chain(lambda e: e.reciprocal(top1[:, :, 0], top1[:, :, 0]))
                flat = "p t e -> p (t e)"
                m_in = matmul(bank[0][:, 0:NTT * E], [(tri[:, :], hot[:, :, :].rearrange(flat))], m_hot)
                m_tot = matmul(bank[1][:, 0:NTT * E], [(ones[:, :], hot[:, :, :].rearrange(flat))])
                dve.wait(m_tot)
                chain(lambda e: e.memset(pre[0][:, 0:1, :], 0.0))
                chain(lambda e: e.tensor_copy(pre[0][:, 1:NTT, :].rearrange(flat), bank[1][:, 0:(NTT - 1) * E]))
                step, cur = 1, 0
                while step < NTT:
                    a_, n_ = pre[cur], pre[1 - cur]
                    chain(lambda e: e.tensor_copy(n_[:, 0:step, :], a_[:, 0:step, :]))
                    chain(lambda e: e.tensor_tensor(n_[:, step:NTT, :], a_[:, step:NTT, :],
                                                    a_[:, 0:NTT - step, :], ALU.add))
                    step, cur = 2 * step, 1 - cur
                chain(lambda e: e.tensor_tensor(wrk[:, :, :].rearrange(flat), pre[cur][:, :, :].rearrange(flat),
                                                bank[0][:, 0:NTT * E], ALU.add))
                chain(lambda e: e.tensor_scalar(wrk[:, :, :], wrk[:, :, :], float(CAP), None, ALU.is_le))
                chain(lambda e: e.tensor_tensor(wrk[:, :, :], wrk[:, :, :], hot[:, :, :], ALU.mult))
                chain(lambda e: e.tensor_tensor(coef[:, :, :], wrk[:, :, :], top1[:, :, :].to_broadcast(full),
                                                ALU.mult))
                barrier()

            with ExitStack() as ctx:
                w1q = sb(ctx, "w1q", [P, C, D])
                w1k = sb(ctx, "w1k", [P, C, D])
                w1v = sb(ctx, "w1v", [P, C, D])
                wl8 = sb(ctx, "wl8", [P, 8, C, D])
                wfc = sb(ctx, "wfc", [P, C, FF])
                wpr = sb(ctx, "wpr", [P, FF // P, D])
                esel = sb(ctx, "esel", [E, E, P])
                xb = sb(ctx, "xb", [P, C, S])
                cb = sb(ctx, "cb", [P, C, S])
                cs = sb(ctx, "cs", [P, KT, E])
                cT = sb(ctx, "cT", [E, S])
                ye = sb(ctx, "ye", [P, 2, C, S])
                r = sb(ctx, "r", [P, C, S])
                yn = sb(ctx, "yn", [P, C, S])
                sq = sb(ctx, "sq2", [P, C, S])
                std = sb(ctx, "std2", [P, S])
                q1 = sb(ctx, "q1", [P, C, S])
                k1 = sb(ctx, "k1", [P, C, S])
                v1 = sb(ctx, "v1", [P, KT, D])
                p1 = sb(ctx, "p1", [P, 2, S])
                st1 = sb(ctx, "st1", [P, 2, 4])
                pT1 = sb(ctx, "pT1", [P, KT, S])
                hb = sb(ctx, "hb", [P, FF // P, S])
                tf5 = sb(ctx, "tf5", [P, 1])
                for dst, src in ((w1q, "L1q"), (w1k, "L1k"), (w1v, "L1v"), (wfc, "wfcT"), (wpr, "wprT")):
                    load("wb", dst[:, :, :], o(src).rearrange("(c p) n -> p c n", p=P))
                load("wb", wl8[:, :, :, :], o("wlT").rearrange("(h c p) n -> p h c n", p=P, c=C))
                m_w = load("wb", esel[:, :, :], o("esel"))
                nc.sync.wait_ge(m_w.sem, m_w.value)
                barrier()
                for h in range(1, 8):
                    dve(lambda e: e.tensor_tensor(wl8[:, 0], wl8[:, 0], wl8[:, h], ALU.add), dve.count.now())
                dve(lambda e: e.tensor_scalar(tf5[:, :], TF1, 0.2, None, ALU.mult))
                wls = wl8[:, 0]

                with loop("layer1", B) as b:
                    barrier()
                    x_in = load("x1in", xb[:, :, :], x1_dram[bass.ds(b, 1)].rearrange("o c p s -> p (o c) s"))
                    c_in = load("ctx1", cb[:, :, :], o("ctxT")[bass.ds(b, 1)].rearrange("o c p s -> p (o c) s"))
                    m = dve(lambda e: e.tensor_copy(cs[:, :, :], coef[:, bass.ds(b * KT, KT), :]))
                    pe.wait(m)
                    for t in range(KT):
                        last = nc.tensor.transpose(bank[0][0:E, t * P:(t + 1) * P], cs[:, t, :], ident[:, :])
                    m = pe.count.mark(last)
                    m_cT = act(lambda e: e.activation(cT[:, :], bank[0][0:E, :], ACT.Copy), m)
                    acc = [bank[6], bank[7]]
                    pe.wait(m_cT)
                    for c in range(C):
                        nc.tensor.matmul(acc[c][:, :], b12[:, c * P:(c + 1) * P], cT[:, :], start=True, stop=False)
                    m_w, m_a = {}, {}
                    yv = [y1T[:, c, bass.ds(b * S, S)] for c in range(C)]

                    def weigh(x):
                        k = x % 2
                        m = matmul(bank[k][:, :], [(esel[:, x, :], cT[:, :])], m_w.get(x - 2), m_cT)
                        for c in range(C):
                            m_w[x] = dve(lambda e: e.tensor_tensor(ye[:, k, c, :], yv[c], bank[k][:, :], ALU.mult),
                                         m, m_a.get(x - 2))

                    weigh(0)
                    for x in range(E):
                        if x + 1 < E:
                            weigh(x + 1)
                        pe.wait(m_w[x])
                        for c in range(C):
                            for i in range(C):
                                last = nc.tensor.matmul(acc[c][:, :], w12[:, x, i, c * P:(c + 1) * P],
                                                        ye[:, x % 2, i, :], start=False,
                                                        stop=(x == E - 1 and i == C - 1))
                        m_a[x] = pe.count.mark(last)
                    for c in range(C):
                        m = dve(lambda e: e.tensor_tensor(r[:, c, :], yv[c], acc[c][:, :], ALU.add), m_a[E - 1])
                    m_y = layernorm(lambda c: r[:, c, :], lambda c: yn[:, c, :], sq, std, bank[0][:, :],
                                    bank[1][:, :], [m], [], lambda c: col("ln2_g", c), lambda c: col("ln2_b", c))
                    dve.wait(x_in)
                    for c in range(C):
                        m = dve(lambda e: e.scalar_tensor_tensor(xb[:, c, :], yn[:, c, :], TF0, xb[:, c, :],
                                                                 ALU.mult, ALU.add), m_y[c])
                    free = {}
                    for c in range(C):
                        mk = matmul(bank[2 + c][:, :], [(w1k[:, i, c * P:(c + 1) * P], cb[:, i, :])
                                                        for i in range(C)], c_in)
                        free[2 + c] = act(lambda e: e.activation(k1[:, c, :], bank[2 + c][:, :], ACT.Identity,
                                                                 bias=col("L1bk", c)), mk)
                    for kt in range(KT):
                        k = 4 + kt % 2
                        mv = matmul(bank[k][:, 0:D], [(cb[:, i, kt * P:(kt + 1) * P], w1v[:, i, :])
                                                      for i in range(C)], free.get(k))
                        free[k] = act(lambda e: e.activation(v1[:, kt, :], bank[k][:, 0:D], ACT.Copy), mv)
                    m_n = layernorm(lambda c: xb[:, c, :], lambda c: yn[:, c, :], sq, std, bank[0][:, :],
                                    bank[1][:, :], [m], [])
                    for c in range(C):
                        mq = matmul(bank[2 + c][:, :], [(w1q[:, i, c * P:(c + 1) * P], yn[:, i, :])
                                                        for i in range(C)], *m_n, free[2 + c])
                        m_q = dve(lambda e: e.tensor_scalar(q1[:, c, :], bank[2 + c][:, :], col("L1bq", c),
                                                            D ** -0.5, ALU.add, ALU.mult), mq)
                    m_S, m_e, m_tr, m_ev = {}, {}, {}, {}
                    for t in range(QB):
                        s = t % 2
                        m_S[t] = matmul(bank[s][:, :], [(q1[:, c, t * P:(t + 1) * P], k1[:, c, :])
                                                        for c in range(C)], m_q, m_e.get(t - 2))
                        m = dve(lambda e: e.tensor_reduce(st1[:, s, 0:1], bank[s][:, :], AXIS_X, ALU.max), m_S[t],
                                m_e.get(t - 2))
                        m = dve(lambda e: e.tensor_scalar(st1[:, s, 1:2], st1[:, s, 0:1], -1.0, None, ALU.mult), m)
                        m_e[t] = act(lambda e: e.activation(p1[:, s, :], bank[s][:, :], ACT.Exp,
                                                            bias=st1[:, s, 1:2], accum_out=st1[:, s, 2:3]),
                                     m, m_tr.get(t - 2))
                        m = dve(lambda e: e.reciprocal(st1[:, s, 3:4], st1[:, s, 2:3]), m_e[t])
                        m = dve(lambda e: e.tensor_scalar(p1[:, s, :], p1[:, s, :], st1[:, s, 3:4], None,
                                                          ALU.mult), m)
                        pe.wait(m, m_ev.get(t - 2), free.get(4 + s))
                        for kt in range(KT):
                            last = nc.tensor.transpose(bank[4 + s][:, kt * P:(kt + 1) * P],
                                                       p1[:, s, kt * P:(kt + 1) * P], ident[:, :])
                        m_tr[t] = pe.count.mark(last)
                        m_ev[t] = act(lambda e: e.activation(
                            pT1[:, :, t * P:(t + 1) * P],
                            bank[4 + s][:, :].rearrange("p (k i) -> p k i", k=KT), ACT.Copy), m_tr[t])
                    zT = sq
                    for c in range(C):
                        m = matmul(bank[6 + c][:, :], [(v1[:, kt, c * P:(c + 1) * P], pT1[:, kt, :])
                                                       for kt in range(KT)], m_ev[3])
                        m_zz = dve(lambda e: e.tensor_scalar(zT[:, c, :], bank[6 + c][:, :], col("L1bv", c), None,
                                                             ALU.add), m)
                    for c in range(C):
                        m = matmul(bank[c][:, :], [(wls[:, i, c * P:(c + 1) * P], zT[:, i, :])
                                                   for i in range(C)], m_zz)
                        m = dve(lambda e: e.tensor_scalar(yn[:, c, :], bank[c][:, :], col("L1bl", c), TX1,
                                                          ALU.add, ALU.mult), m)
                        m_x3 = dve(lambda e: e.tensor_tensor(xb[:, c, :], xb[:, c, :], yn[:, c, :], ALU.add), m)
                    m_n = layernorm(lambda c: xb[:, c, :], lambda c: yn[:, c, :], sq, std, bank[6][:, :],
                                    bank[7][:, :], [m_x3], [])
                    free = {}
                    m_h = []
                    for i in range(FF // P):
                        k = 2 + i % 2
                        m = matmul(bank[k][:, :], [(wfc[:, c, i * P:(i + 1) * P], yn[:, c, :]) for c in range(C)],
                                   *m_n, free.get(k))
                        m = free[k] = act(lambda e: e.activation(hb[:, i, :], bank[k][:, :], ACT.Relu), m)
                        m_h.append(dve(lambda e: e.tensor_tensor(hb[:, i, :], hb[:, i, :], hb[:, i, :],
                                                                 ALU.mult), m))
                    mem, cur, cnt = yn, r, sq
                    for c in range(C):
                        m = matmul(bank[4 + c][:, :], [(wpr[:, i, c * P:(c + 1) * P], hb[:, i, :])
                                                       for i in range(FF // P)], m_h[-1])
                        m_y = dve(lambda e: e.tensor_copy(cur[:, c, :], bank[4 + c][:, :]), m)
                        m = dve(lambda e: e.tensor_copy(mem[:, c, :], bank[4 + c][:, :]), m)
                    dve(lambda e: e.tensor_scalar(cnt[:, :, :], mem[:, :, :], 1.0, None, ALU.is_gt),
                        dve.count.now())
                    mv, cv, yv2, kv = (a[:, :, :].rearrange("p c s -> p (c s)") for a in (mem, cur, q1, cnt))
                    for _ in range(4):
                        dve(lambda e: e.scalar_tensor_tensor(yv2, mv, 0.9, cv, ALU.mult, ALU.add),
                            dve.count.now())
                        dve(lambda e: e.scalar_tensor_tensor(mv, mv, 1.0, yv2, ALU.is_gt, ALU.subtract,
                                                             reverse1=True), dve.count.now())
                        dve(lambda e: e.scalar_tensor_tensor(kv, mv, 1.0, kv, ALU.is_gt, ALU.add),
                            dve.count.now())
                    m = dve(lambda e: e.scalar_tensor_tensor(xb[:, :, :], cnt[:, :, :], tf5[:, 0:1], xb[:, :, :],
                                                             ALU.mult, ALU.add), dve.count.now())
                    out_m = load("out", o("out")[bass.ds(b, 1)].rearrange("o c p s -> p (o c) s"), xb[:, :, :], m)
                    nc.sync.wait_ge(out_m.sem, out_m.value)
                    barrier()


COLS = [(n, c) for n, k in (("bq", 8), ("bk", 8), ("bv", 8), ("bo", 2), ("b_in", 6), ("b_out", 2),
                            ("ln1_g", 2), ("ln1_b", 2), ("ln2_g", 2), ("ln2_b", 2), ("L1bq", 2), ("L1bk", 2),
                            ("L1bv", 2), ("L1bl", 2), ("pix_freq", 1), ("sep_freq", 1), ("phase1", 1),
                            ("phase2", 1), ("a_high", 1), ("a_low", 1), ("b_high", 1), ("b_low", 1),
                            ("quarter", 1)) for c in range(k)]


def shape_constants():
    f = np.float32
    dims = [1.0, WAVE ** -0.5]
    p = np.arange(P)
    const = {"ident": np.eye(P, dtype=f), "fold": (p[:, None] % 32 == p[None, :] % 32).astype(f),
             "tri": (p[:, None] <= p[None, :]).astype(f),
             "rank": np.tile(np.arange(E, 0, -1, dtype=f), (P, 1)),
             "mask": np.where(p[:, None] % 16 == p[None, :] % 16, 0.0, MASKED).astype(f)}
    esel = np.zeros((E, E, P), f)
    for e in range(E):
        esel[e, e, :] = 1.0
    const["esel"] = esel
    row, block = (p % 32) % SEP, (p % 32) // SEP
    used = (p % 32) < 3 * SEP
    trig = used & (row < 8)
    col = {}
    col["pix_freq"] = np.array([100.0 * dims[(i // 32) % 2] / (2 * math.pi) for i in p])
    col["sep_freq"] = np.where(trig, [100.0 * dims[(r // 2) % 2] / (2 * math.pi) for r in row], 0.0)
    cos_row = row % 2 == 0
    col["phase1"] = np.where(used & cos_row, 0.25, 0.0)
    col["phase2"] = np.where(trig & ~cos_row, -0.25, 0.0)
    col["a_high"] = (used & (block != 1)).astype(f)
    col["a_low"] = (used & (block == 1)).astype(f)
    col["b_high"] = (used & (block != 2)).astype(f)
    col["b_low"] = (used & (block == 2)).astype(f)
    col["quarter"] = np.full(P, TURN / 4)
    sel = np.zeros((4, 2, P), f)
    for i in p:
        y = i // 64
        sel[y, 0, i] = sel[2 + y, 0, i] = 1.0
        if trig[i]:
            y = row[i] // 4
            sel[y, 1, i], sel[2 + y, 1, i] = -1.0, 1.0
    const["sel"] = sel
    return const, {k: np.asarray(v, f) for k, v in col.items()}


def kernel(**inputs):
    import concourse.bacc as bacc
    from concourse.bass_utils import run_bass_kernel_spmd

    v = {k: np.asarray(a) for k, a in inputs.items()}
    const, col = shape_constants()

    def chunks(a):
        return a.reshape(-1, P).T

    def features_first(a):
        return np.ascontiguousarray(a.transpose(0, 2, 1)).reshape(B, C, P, S)

    per_partition = {
        "bq": v["L0_xattn_bq"], "bk": v["L0_xattn_bk"], "bv": v["L0_xattn_bv"], "bo": v["L0_xattn_bo"],
        "b_in": v["L0_ffn_in_proj_b"], "b_out": v["L0_ffn_out_proj_b"], "ln1_g": v["L0_ffn_ln1_g"],
        "ln1_b": v["L0_ffn_ln1_b"], "ln2_g": v["L0_ffn_ln2_g"], "ln2_b": v["L0_ffn_ln2_b"],
        "L1bq": v["L1_xattn_bQ"], "L1bk": v["L1_xattn_bK"], "L1bv": v["L1_xattn_bV"], "L1bl": v["L1_xattn_bl"],
    }
    cols = np.empty((P, len(COLS)), np.float32)
    for k, (name, c) in enumerate(COLS):
        cols[:, k] = chunks(per_partition[name])[:, c] if name in per_partition else col[name]

    wg = v["L0_xattn_Wg"]
    feature = np.arange(P) // 32
    rel_w = np.stack([wg[:, feature].T, wg[:, 8 + feature].T], 1)
    sep_w = np.zeros((P, 2, HG), np.float32)
    for i in range(P):
        row = (i % 32) % SEP
        if i % 32 < 3 * SEP:
            heads = np.arange(HG) * 4 + i // 32
            if row < 8:
                sep_w[i, 0], sep_w[i, 1] = wg[heads, 12 + row // 2], wg[heads, 4 + row // 2]
            else:
                sep_w[i, 0] = v["L0_xattn_bg"][heads]
    boxes = v["fside_BxSx4_0"]
    by_query = boxes.reshape(B, NT, 32, 4)
    box_lo, box_hi = (np.stack([by_query[..., k + g // 2] for g in range(4)], 0)
                      .transpose(0, 3, 1, 2).reshape(P, B * NT) for k in (0, 2))
    b1x = np.zeros((E, P, FF // P, E), np.float32)
    for e in range(E):
        b1x[e, :, :, e] = v["L0_ffn_b1"][e].reshape(FF // P, P).T
    arrays = {
        **const, "cols": cols, "gates": np.concatenate([v["g_xattn"], v["g_ffn"]]),
        "xT": features_first(v["x"]), "ctxT": features_first(v["ctx_1024"]),
        "boxT": boxes.transpose(0, 2, 1), "box_lo": box_lo, "box_hi": box_hi, "rel_w": rel_w, "sep_w": sep_w,
        "wqT": v["L0_xattn_Wq"].T, "wkT": v["L0_xattn_Wk"].T, "wvT": v["L0_xattn_Wv"].T, "woT": v["L0_xattn_Wo"].T,
        "in_wT": v["L0_ffn_in_proj_w"].T, "out_wT": v["L0_ffn_out_proj_w"].T, "wg": v["L0_ffn_wg"],
        "w1T": v["L0_ffn_w1"].transpose(0, 2, 1), "w2": v["L0_ffn_w2"], "b1x": b1x, "b2": v["L0_ffn_b2"],
        "L1q": v["L1_xattn_WQ"].T, "L1k": v["L1_xattn_WK"].T, "L1v": v["L1_xattn_WV"].T,
        "wlT": v["L1_xattn_Wl"].T, "wfcT": v["L1_ffn_W_fc"].T, "wprT": v["L1_ffn_W_proj"].T,
    }
    arrays = {k: np.ascontiguousarray(a) for k, a in arrays.items()}

    def program(table):
        nc = bacc.Bacc("TRN2", target_bir_lowering=False, num_devices=1)
        io = {k: nc.dram_tensor("in_" + k, a.shape, mybir.dt.from_np(a.dtype), kind="ExternalInput").ap()
              for k, a in arrays.items()}
        io["out"] = nc.dram_tensor("out_0", (B, C, P, S), F32, kind="ExternalOutput").ap()
        build(nc, table, io)
        return nc

    table = {"per": {}, "names": {}, "new_per": {}, "new_names": {}}
    program(table)
    table["per"], table["names"] = table["new_per"], table["new_names"]
    table["new_per"], table["new_names"] = {}, {}
    nc = program(table)
    assert table["per"] == table["new_per"] and table["names"] == table["new_names"]
    r = run_bass_kernel_spmd(nc, [{"in_" + k: a for k, a in arrays.items()}], core_ids=[0])
    out = r.results[0]["out_0"]
    return np.ascontiguousarray(out.reshape(B, D, S).transpose(0, 2, 1))
```

```python
import math
from contextlib import ExitStack, contextmanager

import numpy as np

import concourse.bass as bass
from concourse import mybir

F32 = mybir.dt.float32
F16 = mybir.dt.float16
ALU = mybir.AluOpType
ACT = mybir.ActivationFunctionType
AXIS_X = mybir.AxisListType.X

P = 128
B, S, D = 8, 512, 256
C = D // P
T = B * S
H0, DK = 16, 64
PAIRS = H0 // 2
QUADS = H0 // 4
HT, QT = 8, 16
HG = H0 // HT
QB = S // P
NT = S // QT
NJ = P // QT
KT = S // P
HM, DM = 4, 64
E, FF = 8, 1024
CAP = T // E
WAVE = 1000.0
TURN = 6.283185
ROUND = 12582912.0
WSCALE = 64.0
CLIP = 1e-6
EPS = 1e-5
MASKED = -1e30
SEP = 9


class Mark:

    def __init__(self, sem, value, order=0):
        self.sem, self.value, self.order = sem, value, order


def latest(marks):
    by_sem = {}
    for m in marks:
        if m is not None and (m.sem not in by_sem or by_sem[m.sem].order < m.order):
            by_sem[m.sem] = m
    return by_sem.values()


class Counter:

    def __init__(self, nc, name, table, prime=0):
        self.name, self.sem, self.table = name, nc.alloc_semaphore(name), table
        self.base, self.k, self.frames = prime, 0, []
        self.total = 0

    def enter(self, loop, i):
        per = self.table["per"].get((loop, self.name), 1)
        self.frames.append((loop, self.base, self.k, per, self.total))
        self.base, self.k = (self.base + self.k) + i * per if per else self.base + self.k, 0

    def leave(self, rounds):
        loop, base, k, _, _ = self.frames.pop()
        per = self.table["new_per"][(loop, self.name)] = self.k
        self.base, self.k = base, k + rounds * per
        self.left = per, self.k

    def mark(self, ins, name=None, step=1):
        ins.then_inc(self.sem, step)
        self.k += step
        self.total += step
        if name is not None:
            self.name_last(name)
        return Mark(self.sem, self.base + self.k, self.total)

    def name_last(self, name):
        self.table["new_names"][(self.name, name)] = self.k

    def now(self):
        return Mark(self.sem, self.base + self.k, self.total)

    def before(self, name):
        per, entered = self.frames[-1][3:]
        k = self.table["names"].get((self.name, name), 1) - per
        return Mark(self.sem, self.base + k, entered + k)

    def after_loop(self, name):
        k = self.left[1] + self.table["names"].get((self.name, name), 1) - self.left[0]
        return Mark(self.sem, self.base + k, self.total - self.k + k)


class Engine:

    def __init__(self, nc, name, eng, table, prime):
        self.e = eng
        self.count = Counter(nc, name, table, prime)
        if prime:
            eng.sem_inc(self.count.sem, prime)

    def wait(self, *marks):
        for m in latest(marks):
            self.e.wait_ge(m.sem, m.value)

    def __call__(self, ins_of, *marks, name=None):
        self.wait(*marks)
        return self.count.mark(ins_of(self.e), name)


def build(nc, table, io):
    o = io.__getitem__
    PRIME = 1200
    pe = Engine(nc, "pe", nc.tensor, table, PRIME)
    act = Engine(nc, "act", nc.scalar, table, PRIME)
    dve = Engine(nc, "dve", nc.vector, table, PRIME)
    pool = Engine(nc, "pool", nc.gpsimd, table, PRIME)
    dmas = {}
    written = nc.alloc_semaphore("written")

    def dma_counter(name):
        if name not in dmas:
            dmas[name] = Counter(nc, "dma_" + name, table)
            assert not loops, name
        return dmas[name]

    loops = []

    @contextmanager
    def loop(name, n):
        with nc.Fori(0, n) as i:
            loops.append(name)
            every = [pe.count, act.count, dve.count, pool.count, *dmas.values()]
            for c in every:
                c.enter(name, i)
            yield i
            for c in every:
                c.leave(n)
            loops.pop()

    def load(name, dst, src, *marks, eng=None):
        q = eng or nc.sync
        for m in latest(marks):
            q.wait_ge(m.sem, m.value)
        return dma_counter(name).mark(q.dma_start(dst, src), step=16)

    for name in ("const", "wx", "x", "xres", "ctx", "x1out", "w1_0", "w1_1", "x1all", "win", "wb2", "w1l", "wb",
                 "x1in0", "x1in1", "ctx10", "ctx11",
                 "out0", "out1"):
        dma_counter(name)

    def barrier():
        nc.all_engine_barrier()

    def sb(ctx, name, shape, dt=F32):
        return ctx.enter_context(nc.sbuf_tensor(name, shape, dt))

    x1_dram = nc.dram_tensor("x1_scratch", (B, C, P, S), F32, kind="Internal").ap()

    with ExitStack() as top:
        bank = [top.enter_context(nc.psum_tensor(f"bank{i}", [P, 512], F32)) for i in range(8)]

        ident = sb(top, "ident", [P, P])
        ones_mean = sb(top, "ones_mean", [P, P])
        gates = sb(top, "gates", [P, 4])
        tanh_g = sb(top, "tanh_g", [P, 4])
        cols = sb(top, "cols", [P, len(COLS)])
        eps_col = sb(top, "eps_col", [P, 1])

        def col(name, c=0):
            k = COLS.index((name, c))
            return cols[:, k:k + 1]

        load("const", ident[:, :], o("ident"))
        load("const", cols[:, :], o("cols"))
        c_in = load("const", gates[:, :], o("gates").partition_broadcast(P))
        ones_m = dve(lambda e: e.memset(ones_mean[:, :], 1.0 / D))
        dve(lambda e: e.memset(eps_col[:, :], EPS))
        act(lambda e: e.activation(tanh_g[:, :], gates[:, :], ACT.Tanh), c_in)
        barrier()
        TX0, TX1, TF0, TF1 = (tanh_g[:, i:i + 1] for i in range(4))

        def matmul(out, pairs, *marks, name=None):
            pe.wait(*marks)
            for n, (lhsT, rhs) in enumerate(pairs):
                last = nc.tensor.matmul(out, lhsT, rhs, start=(n == 0), stop=(n == len(pairs) - 1))
            return pe.count.mark(last, name)

        def interleave(*streams):
            left = list(streams)
            while left:
                for pair in list(left):
                    for _ in range(pair[1]):
                        if next(pair[0], left) is left:
                            left.remove(pair)
                            break

        def later(turns, steps):
            for _ in range(turns):
                yield
            yield from steps

        def layernorm(src, dst, sq, std, mean_ps, var_ps, ready, free, scale=None, shift=None,
                      shaped=lambda a: a):
            out = []
            for _ in layernorm_steps(src, dst, sq, std, mean_ps, var_ps, ready, free, scale, shift, shaped, out):
                pass
            return out

        def layernorm_steps(src, dst, sq, std, mean_ps, var_ps, ready, free, scale=None, shift=None,
                            shaped=lambda a: a, out=None):
            m_mean = matmul(mean_ps, [(ones_mean[:, :], src(c)) for c in range(C)], *ready, *free)
            yield
            m_sq = []
            for c in range(C):
                m_c = dve(lambda e: e.tensor_tensor(shaped(dst(c)), src(c), shaped(mean_ps), ALU.subtract), m_mean)
                m_sq.append(act(lambda e: e.activation(sq[:, c, :], dst(c), ACT.Square), m_c))
            yield
            m_var = matmul(var_ps, [(ones_mean[:, :], sq[:, c, :]) for c in range(C)], m_sq[-1])
            m_std = act(lambda e: e.activation(std[:, :], var_ps, ACT.Sqrt, bias=eps_col[:, 0:1]), m_var)
            yield
            m_r = dve(lambda e: e.reciprocal(std[:, :], std[:, :]), m_std)
            for c in range(C):
                m = dve(lambda e: e.tensor_tensor(dst(c), dst(c), std[:, :], ALU.mult), m_r)
                if scale is not None:
                    m = dve(lambda e: e.tensor_scalar(dst(c), dst(c), scale(c), shift(c), ALU.mult, ALU.add), m)
                out.append(m)
            yield

        with ExitStack() as ctx:
            wq = sb(ctx, "wq", [P, C, H0 * DK])
            wk = sb(ctx, "wk", [P, C, H0 * DK])
            wv = sb(ctx, "wv", [P, C, H0 * DK])
            wo = sb(ctx, "wo", [P, PAIRS, D])
            rel_w = sb(ctx, "rel_w", [P, H0])
            sep_w = sb(ctx, "sep_w", [P, 2, QUADS])
            fold = sb(ctx, "fold", [P, QT])
            kron = sb(ctx, "kron", [P, 2, H0, QT], F16)
            kron_w = sb(ctx, "kron_w", [P, QT])
            sel = sb(ctx, "sel", [4, 2, P])
            centre = sb(ctx, "centre", [P, B * NT])
            inv_size = sb(ctx, "inv_size", [P, B * NT])
            cen_b = sb(ctx, "cen_b", [P, 2, NT])
            xin = sb(ctx, "xin", [P, C, S])
            xres = sb(ctx, "xres", [P, C, S])
            bo_g = sb(ctx, "bo_g", [P, C])
            bq_s = sb(ctx, "bq_s", [P, PAIRS])
            cin = sb(ctx, "cin", [P, C, S])
            box = sb(ctx, "box", [4, S])
            kT = sb(ctx, "kT", [P, 2, PAIRS, S], F16)
            qT = sb(ctx, "qT", [P, PAIRS, S])
            vv = sb(ctx, "vv", [P, KT, H0 * DK])
            feat = sb(ctx, "feat", [P, NT, 2, S], F16)
            feat32 = feat[:, :, :, :].rearrange("p j x s -> p j (x s)").bitcast(F32)
            box_lo, box_hi = (feat32[:, i, 0:B * NT] for i in range(2))
            sepA = sb(ctx, "sepA", [P, QUADS, S], F16)
            sepB = sb(ctx, "sepB", [P, S], F16)
            qbd = sb(ctx, "qbd", [P, HG, 2, HT // 2, NJ, 2 * QT], F16)
            abd = sb(ctx, "abd", [P, HG, NJ, HT, QT], F16)
            ptT = sb(ctx, "ptT", [P, 2, KT, HT, 64])
            eb = sb(ctx, "eb", [P, 2, S])
            pb = sb(ctx, "pb", [P, 2, S])
            small = sb(ctx, "small", [P, 2, 4])
            sep_tmp = sb(ctx, "sep_tmp", [P, S])
            xn = ptT[:, 0, 0:2, :, :].rearrange("p a h q -> p a (h q)")
            lnsq = ptT[:, 0, 2:4, :, :].rearrange("p a h q -> p a (h q)")
            fb = [ptT[:, 1, i, :, :].rearrange("p h q -> p (h q)") for i in range(4)]
            whole = ptT[:, 1, :, :, :].rearrange("p a h q -> p a (h q)")
            std = eb[:, 0, :]
            rb = eb[:, 1, :]
            sa, sbb = pb[:, 0, :], pb[:, 1, :]
            sl, sl2 = sep_tmp[:, :], std

            for dst, src in ((wq, "wqT"), (wk, "wkT"), (wv, "wvT"), (wo, "woT")):
                load("wx", dst[:, :, :], o(src).rearrange("(c p) n -> p c n", p=P))
            load("wx", rel_w[:, :], o("rel_w"))
            load("wx", sep_w[:, :, :], o("sep_w"))
            load("wx", fold[:, :], o("fold"))
            load("wx", sel[:, :, :], o("sel"))
            load("wx", box_lo, o("box_lo"))
            wx = load("wx", box_hi, o("box_hi"))

            bq = COLS.index(("bq", 0))
            dve(lambda e: e.tensor_scalar(bq_s[:, :], cols[:, bq:bq + PAIRS], DK ** -0.5, None, ALU.mult))
            for c in range(C):
                dve(lambda e: e.tensor_tensor(bo_g[:, c:c + 1], col("bo", c), TX0, ALU.mult))
            m = dve(lambda e: e.tensor_tensor(centre[:, :], box_lo, box_hi, ALU.add), wx)
            dve(lambda e: e.tensor_scalar(centre[:, :], centre[:, :], 0.5, None, ALU.mult), m)
            m = dve(lambda e: e.tensor_tensor(inv_size[:, :], box_hi, box_lo, ALU.subtract))
            m = dve(lambda e: e.tensor_scalar(inv_size[:, :], inv_size[:, :], 1.0, None, ALU.add), m)
            dve(lambda e: e.reciprocal(inv_size[:, :], inv_size[:, :]), m)
            dve(lambda e: e.tensor_scalar(sep_w[:, :, :], sep_w[:, :, :], WSCALE, None, ALU.mult), wx)
            m_rw = dve(lambda e: e.tensor_scalar(rel_w[:, :], rel_w[:, :], WSCALE, None, ALU.mult), wx)
            for h in range(H0):
                m = dve(lambda e: e.tensor_scalar(kron_w[:, :], fold[:, :], rel_w[:, h:h + 1], None, ALU.mult),
                        m_rw, dve.count.now())
                m = dve(lambda e: e.tensor_copy(kron[:, 0, h, :], kron_w[:, :]), m)
                dve(lambda e: e.tensor_tensor(kron[:, 1, h, :], kron_w[:, :], kron[:, 0, h, :], ALU.subtract), m)
            pool(lambda e: e.memset(qbd[:, :, :, :, :, :], 0.0))
            pool(lambda e: e.memset(abd[:, :, :, :, :], 0.0))
            barrier()

            bank_free = [None] * 8

            def load_next(b):
                load("x", xin[:, :, :], o("xT")[bass.ds(b, 1)].rearrange("o c p s -> p (o c) s"))
                load("x", box[:, :], o("boxT")[bass.ds(b, 1)].rearrange("o k s -> (o k) s"))
                load("ctx", cin[:, :, :], o("ctxT")[bass.ds(b, 1)].rearrange("o c p s -> p (o c) s"))

            def keys(banks):
                for i in range(PAIRS):
                    k = banks[i % 2]
                    m = matmul(bank[k][:, :], [(wk[:, c, i * P:(i + 1) * P], cin[:, c, :]) for c in range(C)],
                               dmas["ctx"].now(), bank_free[k])
                    m = act(lambda e: e.activation(kT[:, 0, i, :], bank[k][:, :], ACT.Identity,
                                                   bias=col("bk", i)), m)
                    bank_free[k] = dve(lambda e: e.scalar_tensor_tensor(
                        kT[:, 1, i, :], bank[k][:, :], col("bk", i), kT[:, 0, i, :], ALU.add, ALU.subtract), m)
                    yield

            def values_by_key(banks):
                for i in range(2 * KT):
                    kt, n, k = i // 2, i % 2, banks[i % 2]
                    m = matmul(bank[k][:, :], [(cin[:, c, kt * P:(kt + 1) * P], wv[:, c, n * 512:(n + 1) * 512])
                                               for c in range(C)], dmas["ctx"].now(), bank_free[k])
                    bank_free[k] = act(lambda e: e.activation(vv[:, kt, n * 512:(n + 1) * 512], bank[k][:, :],
                                                              ACT.Copy), m)
                    yield

            def queries(banks, heads_read):
                m_xn = []
                yield from layernorm_steps(lambda c: xin[:, c, :], lambda c: xn[:, c, :], lnsq, std,
                                           bank[banks[0]][:, :], bank[banks[1]][:, :], [dmas["x"].now()],
                                           [bank_free[k] for k in banks], out=m_xn)
                for i in range(PAIRS):
                    k = banks[i % 2]
                    m = matmul(bank[k][:, :], [(wq[:, c, i * P:(i + 1) * P], xn[:, c, :]) for c in range(C)],
                               *m_xn, bank_free[k])
                    bank_free[k] = act(lambda e: e.activation(qT[:, i, :], bank[k][:, :], ACT.Identity,
                                                              bias=bq_s[:, i:i + 1], scale=DK ** -0.5),
                                       m, *heads_read)
                    yield

            def features(b, banks):
                k0, k1 = banks
                m = matmul(bank[k0][:, :], [(sel[:, 0, :], box[:, :])], dmas["x"].now(), bank_free[k0])
                m_rb = bank_free[k0] = dve(lambda e: e.tensor_scalar(rb, bank[k0][:, :], 0.5, None, ALU.mult), m)
                m_size = matmul(bank[k1][:, :], [(sel[:, 1, :], box[:, :])], bank_free[k1])
                yield
                m = dve(lambda e: e.tensor_scalar(cen_b[:, 0, :], centre[:, bass.ds(b * NT, NT)], -1.0, None,
                                                  ALU.mult))
                m_c = dve(lambda e: e.tensor_copy(cen_b[:, 1, :], inv_size[:, bass.ds(b * NT, NT)]))
                act.wait(m_rb, m_c)
                m_ln = bank_free[k1] = act(lambda e: e.activation(sl, bank[k1][:, :], ACT.Ln, bias=1.0), m_size)
                yield

                def clip(j0):
                    for j in range(j0, j0 + 4):
                        m = act(lambda e: e.activation(feat32[:, j, :], rb, ACT.Abs, bias=cen_b[:, 0, j:j + 1]))
                        m = dve(lambda e: e.tensor_scalar(feat32[:, j, :], feat32[:, j, :],
                                                          cen_b[:, 1, j:j + 1], 1e-3, ALU.mult, ALU.max), m)
                    return m

                def wrap(j0, m, free):
                    quad = feat32[:, j0:j0 + 4, :]
                    m = dve(lambda e: e.tensor_scalar(quad, quad, col("pix_freq"), col("pix_phase"),
                                                      ALU.mult, ALU.add), m)
                    m = dve(lambda e: e.tensor_scalar(whole, quad, ROUND, -ROUND, ALU.add, ALU.add), m, *free)
                    return [engine(lambda e: e.tensor_tensor(quad[:, part], quad[:, part], whole[:, part],
                                                             ALU.subtract), m)
                            for engine, part in ((dve, slice(0, 2)), (pool, slice(2, 4)))]

                m_clip = clip(0)
                yield
                m_wrap = []
                for j0 in range(0, NT, 4):
                    m = act(lambda e: e.activation(feat32[:, j0:j0 + 4, :], feat32[:, j0:j0 + 4, :], ACT.Ln),
                            m_clip)
                    yield
                    if j0 + 4 < NT:
                        m_clip = clip(j0 + 4)
                    m_wrap = wrap(j0, m, m_wrap)
                    yield
                m = dve(lambda e: e.tensor_scalar(sl, sl, col("sep_freq"), None, ALU.mult), m_ln)
                sep_m = []
                for phase, dst, tmp in ((col("phase1"), sa, fb[0]), (col("phase2"), sbb, fb[1])):
                    mp = dve(lambda e: e.tensor_scalar(dst, sl, phase, None, ALU.add), m)
                    mp = dve(lambda e: e.tensor_scalar(tmp, dst, ROUND, -ROUND, ALU.add, ALU.add), mp)
                    mp = dve(lambda e: e.tensor_tensor(dst, dst, tmp, ALU.subtract), mp)
                    sep_m.append(act(lambda e: e.activation(dst, dst, ACT.Sin, scale=TURN), mp))
                yield
                act.wait(dve.count.now(), pool.count.now())
                m_low = {}
                sep = separable(sep_m)
                for j in range(NT):
                    tmp = fb[j % 4]
                    m = act(lambda e: e.activation(tmp, feat32[:, j, :], ACT.Sin, scale=TURN), m_low.get(j - 4))
                    if j % 8 in HIGH_ACT:
                        m = act(lambda e: e.activation(feat[:, j, 0, :], tmp, ACT.Copy), m)
                    else:
                        m = dve(lambda e: e.tensor_copy(feat[:, j, 0, :], tmp), m)
                    low = dve if j % 8 in LOW_DVE else pool
                    m_low[j] = low(lambda e: e.tensor_tensor(feat[:, j, 1, :], tmp, feat[:, j, 0, :],
                                                             ALU.subtract), m)
                    if j % 2:
                        next(sep, None)
                    yield
                for _ in sep:
                    pass

            def separable(sep_m):
                m = dve(lambda e: e.tensor_copy(sepB[:, :], sa), sep_m[0])
                m = dve(lambda e: e.tensor_tensor(sl, sa, sepB[:, :], ALU.subtract), m)
                yield
                m = dve(lambda e: e.tensor_scalar(sl, sl, col("b_low"), None, ALU.mult), m)
                m = dve(lambda e: e.scalar_tensor_tensor(sepB[:, :], sepB[:, :], col("b_high"), sl,
                                                         ALU.mult, ALU.add), m)
                yield
                for g in range(QUADS):
                    m = dve(lambda e: e.tensor_scalar(sl, sa, sep_w[:, 0, g:g + 1], None, ALU.mult), m)
                    m = dve(lambda e: e.scalar_tensor_tensor(sl, sbb, sep_w[:, 1, g:g + 1], sl,
                                                             ALU.mult, ALU.add), m, sep_m[1])
                    yield
                    m = dve(lambda e: e.tensor_copy(sepA[:, g, :], sl), m)
                    m = dve(lambda e: e.tensor_tensor(sl2, sl, sepA[:, g, :], ALU.subtract), m)
                    yield
                    m = dve(lambda e: e.tensor_scalar(sl2, sl2, col("a_low"), None, ALU.mult), m)
                    m = dve(lambda e: e.scalar_tensor_tensor(sepA[:, g, :], sepA[:, g, :], col("a_high"), sl2,
                                                             ALU.mult, ALU.add), m)
                    yield

            def project_out(b, read):
                for c in range(C):
                    read.append(matmul(bank[c][:, :], [(wo[:, i, c * P:(c + 1) * P], qT[:, i, :])
                                                       for i in range(PAIRS)], bank_free[c]))
                yield
                m_res = []
                for c in range(C):
                    m = dve(lambda e: e.scalar_tensor_tensor(xres[:, c, :], bank[c][:, :], TX0, xres[:, c, :],
                                                             ALU.mult, ALU.add), read[c], dmas["xres"].now())
                    bank_free[c] = m
                    m_res.append(dve(lambda e: e.tensor_scalar(xres[:, c, :], xres[:, c, :], bo_g[:, c:c + 1], None,
                                                               ALU.add), m))
                    yield
                load("x1out", x1_dram[bass.ds(b, 1)].rearrange("o c p s -> p (o c) s"), xres[:, :, :], *m_res)

            def block_diagonals(g, q, done, *marks):
                out = []
                for h in range(2):
                    if not h:
                        act.wait(*marks)
                        dve.wait(*marks)
                    rows = slice(64 * h, 64 * h + 64)
                    src = (qT[rows, 4 * g:4 * g + 4, bass.ds(q * P, P)].rearrange("p a (j i) -> p a j i", i=QT))
                    high, low = (qbd[rows, g, w, :, :, QT * h:QT * h + QT] for w in range(2))
                    m = act(lambda e: e.activation(high, src, ACT.Copy))
                    yield
                    out.append(dve(lambda e: e.tensor_tensor(low, src, high, ALU.subtract), m,
                                   name=f"bd{g}" if h else None))
                by_quarter = abd[0:32, g, :, :, :].rearrange("p j (u h) i -> p h u j i", h=4)
                for h in range(4):
                    src = (sepA[32 * h:32 * h + 32, 2 * g:2 * g + 2, bass.ds(q * P, P)]
                           .rearrange("p u (j i) -> p u j i", i=QT))
                    m = act(lambda e: e.activation(by_quarter[:, h], src, ACT.Copy), name=f"bd{g}")
                    yield
                done.extend(out + [m])

            def transition(done, b):
                read = []
                last = project_out(done, read) if done is not None else iter(())
                terms, normal = features(b, [4, 5]), queries([6, 7], read)
                for first in [terms, normal, terms, last] + HEAD_START * [terms]:
                    next(first, None)
                interleave((terms, TERM_STEPS), (normal, 1), (keys([2, 3]), 1), (last, 1),
                           (values_by_key([4, 5]), 1))
                for _ in block_diagonals(0, 0, [], dve.count.now(), act.count.now()):
                    pass
                if done is not None:
                    m = dmas["x1out"].now()
                    nc.sync.wait_ge(m.sem, m.value)
                barrier()

            def attention_tiles():
                query_block(0, None)
                with loop("qblock", QB - 1) as n:
                    query_block(n + 1, n)
                query_block(None, QB - 1)

            def query_block(q, before):
                NTILE = HG * NJ
                Sb, Gb, Tb, Ob = bank[0:2], bank[2:4], bank[4:6], bank[6:8]
                m_S, m_G, m_TR, m_exp, m_P, m_ev, m_stt, m_bd, m_pv, m_ov = ({} for _ in range(10))

                def earlier(marks, engine, name, n, count):
                    if n in marks:
                        return marks[n]
                    return last_round(engine, f"{name}{n + count}")

                def last_round(engine, name):
                    if before is None:
                        return None
                    return engine.count.before(name) if q is not None else engine.count.after_loop(name)

                def finish_tile(t):
                    s = t % 2
                    m_stt[t] = dve(lambda e: e.scalar_tensor_tensor(
                        pb[:, s, :], Gb[s][:, :], CLIP * WSCALE, eb[:, s, :], ALU.max, ALU.mult,
                        accum_out=small[:, s, 0:1]), earlier(m_G, pe, "G", t, NTILE),
                        earlier(m_exp, act, "exp", t, NTILE), earlier(m_TR, pe, "tr", t - 2, NTILE),
                        name=f"stt{t}")
                    m = dve(lambda e: e.reciprocal(small[:, s, 1:2], small[:, s, 0:1]), m_stt[t])
                    m_P[t] = dve(lambda e: e.tensor_scalar(pb[:, s, :], pb[:, s, :], small[:, s, 1:2], None,
                                                           ALU.mult), m, name=f"P{t}")

                def transpose_tile(t):
                    s, v = t % 2, t // 4
                    pe.wait(earlier(m_P, dve, "P", t, NTILE), earlier(m_ev, act, "ev", t - 2, NTILE))
                    for kt in range(KT):
                        last = nc.tensor.transpose(Tb[s][:, kt * P:(kt + 1) * P],
                                                   pb[:, s, kt * P:(kt + 1) * P], ident[:, :])
                    m_TR[t] = pe.count.mark(last, f"tr{t}")
                    m_ev[t] = act(lambda e: e.activation(
                        ptT[:, v % 2, :, :, QT * (t % 4):QT * (t % 4 + 1)],
                        Tb[s][:, :].rearrange("p (k h i) -> p k h i", k=KT, h=HT), ACT.Copy),
                        m_TR[t], earlier(m_pv, pe, "pv", v - 2, 4), name=f"ev{t}")

                def values(v, a):
                    out, where, g = Ob[v % 2], before if v < 0 else q, v // 2 % HG
                    if not a:
                        pe.wait(earlier(m_ev, act, "ev", 4 * v + 3, NTILE), earlier(m_ov, dve, "ov", v - 2, 4))
                    for kt in range(KT):
                        for h in range(2):
                            n = 2 * a + h
                            last = nc.tensor.matmul(
                                out[64 * h:64 * h + 64, a * 64:(a + 1) * 64],
                                vv[:, kt, (HT * g + n) * DK:(HT * g + n + 1) * DK],
                                ptT[:, v % 2, kt, n, :], start=(kt == 0), stop=(kt == KT - 1))
                    if a < 3:
                        return
                    m_pv[v] = pe.count.mark(last, f"pv{v}")
                    bv = COLS.index(("bv", 0)) + 4 * g
                    m_ov[v] = dve(lambda e: e.tensor_tensor(
                        qT[:, 4 * g:4 * g + 4, bass.ds(where * P + v % 2 * 64, 64)],
                        out[:, 0:4 * 64].rearrange("p (a q) -> p a q", a=4),
                        cols[:, bv:bv + 4].unsqueeze(2).to_broadcast([P, 4, 64]), ALU.add), m_pv[v], name=f"ov{v}")

                if q is None:
                    finish_tile(-1)
                    transpose_tile(-2)
                    transpose_tile(-1)
                    for t in range(NTILE, NTILE + 6):
                        values((t - 6) // 4 - 4, (t - 6) % 4)
                    return
                m_bd[0] = [last_round(act, "bd0"), last_round(dve, "bd0")]
                for t in range(NTILE):
                    s, g, j = t % 2, t // NJ, t % NJ
                    if j == 0:
                        pe.wait(*m_bd[g])
                    pe.wait(earlier(m_exp, act, "exp", t - 2, NTILE))
                    for w, x in ((0, 0), (0, 1), (1, 0)):
                        for a in range(HT // 2):
                            last = nc.tensor.matmul(Sb[s][32 * a:32 * a + 32, :], qbd[:, g, w, a, j, :],
                                                    kT[:, x, 4 * g + a, :], start=(w == x), stop=(w == 1))
                    m_S[t] = pe.count.mark(last)
                    pe.wait(earlier(m_stt, dve, "stt", t - 2, NTILE))
                    nc.tensor.matmul(Gb[s][:, :], abd[:, g, j, :, :].rearrange("p h i -> p (h i)"), sepB[:, :],
                                     start=True, stop=False)
                    for w, x in ((0, 0), (0, 1), (1, 0)):
                        last = nc.tensor.matmul(
                            Gb[s][:, :], kron[:, w, HT * g:HT * (g + 1), :].rearrange("p h i -> p (h i)"),
                            feat[:, bass.ds(q * NJ + j, 1), x, :].rearrange("p o s -> p (o s)"),
                            start=False, stop=(w == 1))
                    m_G[t] = pe.count.mark(last, f"G{t}")
                    m = dve(lambda e: e.tensor_reduce(small[:, s, 2:3], Sb[s][:, :], AXIS_X, ALU.max),
                            m_S[t], earlier(m_exp, act, "exp", t - 2, NTILE))
                    m = dve(lambda e: e.tensor_scalar(small[:, s, 3:4], small[:, s, 2:3], -1.0, None,
                                                      ALU.mult), m)
                    m_exp[t] = act(lambda e: e.activation(eb[:, s, :], Sb[s][:, :], ACT.Exp,
                                                          bias=small[:, s, 3:4]), m,
                                   earlier(m_stt, dve, "stt", t - 2, NTILE), name=f"exp{t}")
                    if t or before is not None:
                        finish_tile(t - 1)
                    if t >= 2 or before is not None:
                        transpose_tile(t - 2)
                    if t == 1:
                        m_bd[1] = []
                        diagonals = block_diagonals(1, q, m_bd[1], earlier(m_G, pe, "G", -1, NTILE))
                    if t == NJ + 1:
                        for _ in diagonals:
                            pass
                        diagonals = block_diagonals(0, (q + 1) % QB, [], m_G[NJ - 1])
                    if t:
                        next(diagonals, None)
                    if t in (NJ - 1, NTILE - 1):
                        for _ in diagonals:
                            pass
                    if t >= 6 or before is not None:
                        values((t - 6) // 4, (t - 6) % 4)

            def attention():
                attention_tiles()
                barrier()

            def tiles_of(b, more):
                load("xres", xres[:, :, :], o("xT")[bass.ds(b, 1)].rearrange("o c p s -> p (o c) s"))
                if more:
                    load_next(b + 1)
                attention()

            load_next(0)
            transition(None, 0)
            with loop("xattn0", B - 1) as b:
                tiles_of(b, True)
                transition(b, b + 1)
            tiles_of(B - 1, False)
            for _ in project_out(B - 1, []):
                pass
            nc.sync.wait_ge(dmas["x1out"].now().sem, dmas["x1out"].now().value)
            barrier()

        with ExitStack() as outer:
            y1T = sb(outer, "y1T", [P, C, T])
            logits = sb(outer, "logits", [P, T // P, E])
            coef = sb(outer, "coef", [P, T // P, E])
            w12 = sb(outer, "w12", [P, E, C, D])
            b12 = sb(outer, "b12", [E, D])
            w1q = sb(outer, "w1q", [P, C, D])
            w1k = sb(outer, "w1k", [P, C, D])
            w1v = sb(outer, "w1v", [P, C, D])
            wls = sb(outer, "wls", [P, C, D])
            wfc = sb(outer, "wfc", [P, C, FF])
            wpr = sb(outer, "wpr", [P, FF // P, D])
            with ExitStack() as ctx:
                w_in = sb(ctx, "w_in", [P, C, 3 * D])
                w_out = sb(ctx, "w_out", [P, C, D])
                mask = sb(ctx, "mask", [P, P])
                wl8 = sb(ctx, "wl8", [P, 8, C, D])
                m_wb = load("wb", b12[:, :], o("b2"))

                w1e = [sb(ctx, f"w1e{i}", [P, FF // P, D]) for i in range(2)]
                w2e = [sb(ctx, f"w2e{i}", [P, FF // P, D]) for i in range(2)]
                b1e = [sb(ctx, f"b1e{i}", [P, FF // P, E]) for i in range(2)]

                def load_expert(x, i):
                    load(f"w1_{i}", w1e[i][:, :, :], o("w1T")[bass.ds(x, 1)].rearrange("o (k p) d -> p (o k) d", p=P))
                    load(f"w1_{i}", w2e[i][:, :, :], o("w2")[bass.ds(x, 1)].rearrange("o (k p) d -> p (o k) d", p=P))
                    load(f"w1_{i}", b1e[i][:, :, :], o("b1x")[bass.ds(x, 1)].rearrange("o p k e -> p (o k) e"))

                def expert(x, i, more=True):
                    pe.wait(dmas[f"w1_{i}"].now())
                    if more:
                        load_expert(x + 1, 1 - i)
                    for c in range(C):
                        m = matmul(bank[c][:, 0:D], [(w1e[i][:, k, c * P:(c + 1) * P], w2e[i][:, k, :])
                                                     for k in range(FF // P)])
                        act(lambda e: e.activation(w12[:, bass.ds(x, 1), c, :].rearrange("p o d -> p (o d)"),
                                                   bank[c][:, 0:D], ACT.Copy), m)
                    m = matmul(bank[2][0:E, 0:D], [(b1e[i][:, k, :], w2e[i][:, k, :]) for k in range(FF // P)])
                    dve(lambda e: e.tensor_tensor(b12[:, :], b12[:, :], bank[2][0:E, 0:D], ALU.add), m,
                        dve.count.now())
                    barrier()

                load_expert(0, 0)
                for c in range(C):
                    load("x1all", y1T[:, c, :].rearrange("p (b s) -> p b s", b=B),
                         x1_dram[:, c, :, :].rearrange("b p s -> p b s"))
                load("win", w_in[:, :, :], o("in_wT").rearrange("(c p) n -> p c n", p=P))
                load("win", w_out[:, :, :], o("out_wT").rearrange("(c p) n -> p c n", p=P))
                load("win", mask[:, :], o("mask"))
                dve.wait(m_wb)
                expert(0, 0)
                with loop("experts", E // 2 - 1) as n:
                    expert(2 * n + 1, 1)
                    expert(2 * n + 2, 0)
                expert(E - 1, 1, False)

                class Stream:

                    def __init__(self, n):
                        self.n, self.bank = n, bank[4 * n:4 * n + 4]
                        self.z = sb(ctx, f"mha_z{n}", [P, C, 512])
                        self.sq = sb(ctx, f"mha_sq{n}", [P, C, 512])
                        self.std = sb(ctx, f"mha_std{n}", [P, 512])
                        self.qk = sb(ctx, f"mha_qk{n}", [P, 4, 4, P])
                        self.vt = sb(ctx, f"mha_vt{n}", [P, 4, D])
                        self.sm = sb(ctx, f"mha_sm{n}", [P, 2, HM, P])
                        self.pt = sb(ctx, f"mha_pt{n}", [P, 2, HM, P])
                        self.stat = sb(ctx, f"mha_stat{n}", [P, 2, 3, HM])
                        self.oT = sb(ctx, f"mha_oT{n}", [P, C, 512])
                        self.yb = self.oT

                mha_streams = []

                def mha(st, sblk):
                    z, sq, std, qk, vt, sm, pt, stat, oT, yb = (
                        st.z, st.sq, st.std, st.qk, st.vt, st.sm, st.pt, st.stat, st.oT, st.yb)
                    bk = st.bank
                    place = [y1T[:, c, :].rearrange("p (b s) -> p b s", b=B)[:, :, bass.ds(sblk * 64, 64)]
                             .rearrange("p b (t s) -> p t b s", t=4) for c in range(C)]
                    m_z = []
                    yield from layernorm_steps(
                        lambda c: place[c], lambda c: z[:, c, :], sq, std, bk[0][:, :], bk[1][:, :], [], [],
                        shaped=lambda a: a.rearrange("p (t b s) -> p t b s", t=4, b=B), out=m_z)
                    free = {}
                    for i in range(4):
                        k = 2 + i % 2
                        m = matmul(bk[k][:, :], [(w_in[:, c, i * P:(i + 1) * P], z[:, c, :]) for c in range(C)],
                                   *m_z, free.get(k))
                        m_q = free[k] = dve(lambda e: e.tensor_scalar(
                            qk[:, i, :, :].rearrange("p t n -> p (t n)"), bk[k][:, :], col("b_in", i),
                            DM ** -0.5 if i < 2 else 1.0, ALU.add, ALU.mult), m)
                        k = i % 2
                        m = matmul(bk[k][:, 0:D], [(z[:, c, i * P:(i + 1) * P], w_in[:, c, 2 * D:3 * D])
                                                   for c in range(C)], free.get(k))
                        m_v = free[k] = act(lambda e: e.activation(vt[:, i, :], bk[k][:, 0:D], ACT.Copy), m)
                        yield
                    m_sm, m_pt, m_tr, m_pv, m_ov, m_sub = {}, {}, {}, {}, {}, {}

                    def scores(t):
                        s = t % 2
                        pe.wait(m_q, m_sub.get(t - 1), m_v)
                        for h in range(HM):
                            rows = slice(64 * (h % 2), 64 * (h % 2) + 64)
                            at = (h // 2) * P
                            last = nc.tensor.matmul(bk[h % 2][:, at:at + P],
                                                    qk[rows, h // 2, t, :], qk[rows, 2 + h // 2, t, :],
                                                    start=True, stop=True)
                        m = pe.count.mark(last)
                        for h in range(2):
                            m_sub[t] = dve(lambda e: e.tensor_tensor(
                                sm[:, s, h:HM:2, :],
                                bk[h][:, 0:2 * P].rearrange("p (h k) -> p h k", h=2),
                                mask[:, :].unsqueeze(1).to_broadcast([P, 2, P]), ALU.add), m,
                                m_tr.get(t - 2))
                        m = dve(lambda e: e.tensor_reduce(stat[:, s, 0, :], sm[:, s, :, :], AXIS_X, ALU.max),
                                m_sub[t])
                        m = dve(lambda e: e.tensor_scalar(stat[:, s, 0, :], stat[:, s, 0, :], -1.0, None,
                                                          ALU.mult), m)
                        for h in range(HM):
                            m_e = act(lambda e: e.activation(sm[:, s, h, :], sm[:, s, h, :], ACT.Exp,
                                                             bias=stat[:, s, 0, h:h + 1],
                                                             accum_out=stat[:, s, 1, h:h + 1]), m)
                        m_sm[t] = m_e

                    def normalise(t):
                        s = t % 2
                        m = dve(lambda e: e.reciprocal(stat[:, s, 2, :], stat[:, s, 1, :]), m_sm[t])
                        m_sm[t] = dve(lambda e: e.tensor_tensor(
                            sm[:, s, :, :], sm[:, s, :, :],
                            stat[:, s, 2, :].unsqueeze(2).to_broadcast([P, HM, P]), ALU.mult), m)

                    def turn(t):
                        s = t % 2
                        pe.wait(m_sm[t], m_pt.get(t - 1), m_q)
                        for h in range(HM):
                            last = nc.tensor.transpose(bk[2][:, h * P:(h + 1) * P], sm[:, s, h, :], ident[:, :])
                        m_tr[t] = pe.count.mark(last)
                        m_pt[t] = act(lambda e: e.activation(
                            pt[:, s, :, :], bk[2][:, :].rearrange("p (h k) -> p h k", h=HM), ACT.Copy),
                            m_tr[t], m_pv.get(t - 2))

                    def values(t):
                        s = t % 2
                        pe.wait(m_pt[t], m_ov.get(t - 1))
                        for h in range(HM):
                            at = (h // 2) * P
                            last = nc.tensor.matmul(
                                bk[3][64 * (h % 2):64 * (h % 2) + 64, at:at + P],
                                vt[:, t, h * DM:(h + 1) * DM], pt[:, s, h, :], start=True, stop=True)
                        m_pv[t] = pe.count.mark(last)
                        for c in range(C):
                            m_ov[t] = dve(lambda e: e.tensor_scalar(
                                oT[:, c, t * P:(t + 1) * P],
                                bk[3][:, c * P:(c + 1) * P],
                                col("b_in", 4 + c), None, ALU.add), m_pv[t])

                    for t in range(4 + 2):
                        if t < 4:
                            scores(t)
                        if 1 <= t < 5:
                            normalise(t - 1)
                            turn(t - 1)
                        if t >= 2:
                            values(t - 2)
                        yield
                    for c in range(C):
                        m = matmul(bk[c][:, :], [(w_out[:, i, c * P:(c + 1) * P], oT[:, i, :])
                                                 for i in range(C)], m_ov[3])
                        m_r = dve(lambda e: e.scalar_tensor_tensor(z[:, c, :], bk[c][:, :], col("b_out", c),
                                                                   z[:, c, :], ALU.add, ALU.add), m)
                    yield
                    m_y = []
                    yield from layernorm_steps(
                        lambda c: z[:, c, :], lambda c: yb[:, c, :], sq, std, bk[2][:, :], bk[3][:, :], [m_r], [],
                        out=m_y)
                    for c in range(C):
                        dve(lambda e: e.tensor_scalar(
                            place[c], yb[:, c, :].rearrange("p (t b s) -> p t b s", t=4, b=B),
                            col("ln1_g", c), col("ln1_b", c), ALU.mult, ALU.add), m_y[c])

                for i in range(2):
                    mha_streams.append(Stream(i))
                for m in (dmas["x1all"].now(), dmas["win"].now()):
                    nc.sync.wait_ge(m.sem, m.value)
                barrier()
                m_wl = load("w1l", wl8[:, :, :, :], o("wlT").rearrange("(h c p) n -> p h c n", p=P, c=C))
                for dst, src in ((w1q, "L1q"), (w1k, "L1k"), (w1v, "L1v"), (wfc, "wfcT"), (wpr, "wprT")):
                    load("wb", dst[:, :, :], o(src).rearrange("(c p) n -> p c n", p=P))
                with loop("mha", S // 128) as n:
                    a, b = (mha(st, 2 * n + st.n) for st in mha_streams)
                    for _ in range(MHA_LAG):
                        next(a)
                    interleave((a, 1), (b, 1))
                    barrier()
                dve(lambda e: e.tensor_tensor(wls[:, :, :], wl8[:, 0], wl8[:, 1], ALU.add), m_wl)
                for h in range(2, 8):
                    dve(lambda e: e.tensor_tensor(wls[:, :, :], wls[:, :, :], wl8[:, h], ALU.add), dve.count.now())
                m = dmas["wb"].now()
                nc.sync.wait_ge(m.sem, m.value)
                barrier()

            with ExitStack() as ctx:
                wg = sb(ctx, "wg", [P, C, E])
                tri = sb(ctx, "tri", [P, P])
                ones = sb(ctx, "ones", [P, P])
                rank = sb(ctx, "rank", [P, E])
                NTT = T // P
                top1 = sb(ctx, "top1", [P, NTT, 1])
                hot = sb(ctx, "hot", [P, NTT, E])
                wrk = sb(ctx, "wrk", [P, NTT, E])
                pre = [sb(ctx, "pre0", [P, NTT, E]), sb(ctx, "pre1", [P, NTT, E])]
                load("wb2", wg[:, :, :], o("wg").rearrange("(c p) n -> p c n", p=P))
                load("wb2", tri[:, :], o("tri"))
                m_w = load("wb2", rank[:, :], o("rank"))
                dve(lambda e: e.memset(ones[:, :], 1.0))
                nc.sync.wait_ge(m_w.sem, m_w.value)
                barrier()
                for t in range(NTT):
                    for c in range(C):
                        last = nc.tensor.matmul(bank[0][:, t * E:(t + 1) * E], y1T[:, c, t * P:(t + 1) * P],
                                                wg[:, c, :], start=(c == 0), stop=(c == C - 1))
                m = pe.count.mark(last)
                dve(lambda e: e.tensor_copy(logits[:, :, :],
                                            bank[0][:, 0:NTT * E].rearrange("p (t e) -> p t e", t=NTT)), m)

                def chain(ins_of):
                    return dve(ins_of, dve.count.now())

                full = [P, NTT, E]
                chain(lambda e: e.tensor_reduce(top1[:, :, 0], logits[:, :, :], AXIS_X, ALU.max))
                chain(lambda e: e.tensor_tensor(wrk[:, :, :], logits[:, :, :], top1[:, :, :].to_broadcast(full),
                                                ALU.subtract))
                chain(lambda e: e.tensor_scalar(hot[:, :, :], wrk[:, :, :], 0.0, None, ALU.is_equal))
                chain(lambda e: e.tensor_tensor(hot[:, :, :], hot[:, :, :],
                                                rank[:, :].unsqueeze(1).to_broadcast(full), ALU.mult))
                chain(lambda e: e.tensor_reduce(top1[:, :, 0], hot[:, :, :], AXIS_X, ALU.max))
                m_hot = chain(lambda e: e.tensor_tensor(hot[:, :, :], hot[:, :, :],
                                                        top1[:, :, :].to_broadcast(full), ALU.is_equal))
                m = act(lambda e: e.activation(wrk[:, :, :], wrk[:, :, :], ACT.Exp), m_hot)
                dve.wait(m)
                chain(lambda e: e.tensor_reduce(top1[:, :, 0], wrk[:, :, :], AXIS_X, ALU.add))
                chain(lambda e: e.reciprocal(top1[:, :, 0], top1[:, :, 0]))
                flat = "p t e -> p (t e)"
                m_in = matmul(bank[0][:, 0:NTT * E], [(tri[:, :], hot[:, :, :].rearrange(flat))], m_hot)
                m_tot = matmul(bank[1][:, 0:NTT * E], [(ones[:, :], hot[:, :, :].rearrange(flat))])
                dve.wait(m_tot)
                chain(lambda e: e.memset(pre[0][:, 0:1, :], 0.0))
                chain(lambda e: e.tensor_copy(pre[0][:, 1:NTT, :].rearrange(flat), bank[1][:, 0:(NTT - 1) * E]))
                step, cur = 1, 0
                while step < NTT:
                    a_, n_ = pre[cur], pre[1 - cur]
                    chain(lambda e: e.tensor_copy(n_[:, 0:step, :], a_[:, 0:step, :]))
                    chain(lambda e: e.tensor_tensor(n_[:, step:NTT, :], a_[:, step:NTT, :],
                                                    a_[:, 0:NTT - step, :], ALU.add))
                    step, cur = 2 * step, 1 - cur
                chain(lambda e: e.tensor_tensor(wrk[:, :, :].rearrange(flat), pre[cur][:, :, :].rearrange(flat),
                                                bank[0][:, 0:NTT * E], ALU.add))
                chain(lambda e: e.tensor_scalar(wrk[:, :, :], wrk[:, :, :], float(CAP), None, ALU.is_le))
                chain(lambda e: e.tensor_tensor(wrk[:, :, :], wrk[:, :, :], hot[:, :, :], ALU.mult))
                chain(lambda e: e.tensor_tensor(coef[:, :, :], wrk[:, :, :], top1[:, :, :].to_broadcast(full),
                                                ALU.mult))
                barrier()

            with ExitStack() as ctx:
                tf5 = sb(ctx, "tf5", [P, 1])
                tmp, cnt = (sb(ctx, name, [P, C * S]) for name in ("spike_tmp", "spike_cnt"))

                def flat(a):
                    return a[:, :, :].rearrange("p c s -> p (c s)")

                class Stream:

                    def __init__(self, n):
                        self.n, self.bank = n, bank[4 * n:4 * n + 4]
                        self.xb = sb(ctx, f"xb_{n}", [P, C, S])
                        self.cb = sb(ctx, f"cb_{n}", [P, C, S])
                        self.cs = sb(ctx, f"cs_{n}", [P, KT, E])
                        self.cT = sb(ctx, f"cT_{n}", [E, S])
                        self.wide = sb(ctx, f"wide_{n}", [P, 4, S])
                        self.yn = sb(ctx, f"yn_{n}", [P, C, S])
                        self.sq = sb(ctx, f"sq_{n}", [P, C, S])
                        self.std = sb(ctx, f"std_{n}", [P, S])
                        self.q1 = sb(ctx, f"q1_{n}", [P, C, S])
                        self.k1 = sb(ctx, f"k1_{n}", [P, C, S])
                        self.v1 = sb(ctx, f"v1_{n}", [P, KT, D])
                        self.st1 = sb(ctx, f"st1_{n}", [P, 2, 4])
                        self.pT1 = sb(ctx, f"pT1_{n}", [P, KT, S])
                        self.x3 = sb(ctx, f"x3_{n}", [P, C, S])
                        self.y = sb(ctx, f"y_{n}", [P, C, S])
                        self.mem = sb(ctx, f"mem_{n}", [P, C, S])
                        self.spikes_done = None

                streams = [Stream(0), Stream(1)]
                dve(lambda e: e.tensor_scalar(tf5[:, :], TF1, 0.2, None, ALU.mult))
                barrier()

                def layer1(st, b):
                    xb, cb, cs, cT, yn, sq, std, q1, k1, v1, st1, pT1 = (
                        st.xb, st.cb, st.cs, st.cT, st.yn, st.sq, st.std, st.q1, st.k1, st.v1, st.st1, st.pT1)
                    bk, free = st.bank, [None] * 4
                    x_in = load(f"x1in{st.n}", xb[:, :, :], x1_dram[bass.ds(b, 1)].rearrange("o c p s -> p (o c) s"))
                    c_in = load(f"ctx1{st.n}", cb[:, :, :],
                                o("ctxT")[bass.ds(b, 1)].rearrange("o c p s -> p (o c) s"))
                    m = dve(lambda e: e.tensor_copy(cs[:, :, :], coef[:, bass.ds(b * KT, KT), :]))
                    pe.wait(m)
                    for t in range(KT):
                        last = nc.tensor.transpose(bk[0][0:E, t * P:(t + 1) * P], cs[:, t, :], ident[:, :])
                    m = pe.count.mark(last)
                    m_cT = act(lambda e: e.activation(cT[:, :], bk[0][0:E, :], ACT.Copy), m)
                    yield
                    acc = bk[2:4]
                    ye = [st.wide[:, 0:2, :], st.wide[:, 2:4, :]]
                    pe.wait(m_cT)
                    for c in range(C):
                        nc.tensor.matmul(acc[c][:, :], b12[:, c * P:(c + 1) * P], cT[:, :], start=True, stop=False)
                    m_w, m_a = {}, {}
                    yv = [y1T[:, c, bass.ds(b * S, S)] for c in range(C)]

                    def weigh(x):
                        k = x % 2
                        m = matmul(bk[k][:, :], [(ident[0:E, x:x + 1].to_broadcast([E, P]), cT[:, :])], m_w.get(x - 2), m_cT)
                        for c in range(C):
                            m_w[x] = dve(lambda e: e.tensor_tensor(ye[k][:, c, :], yv[c], bk[k][:, :], ALU.mult),
                                         m, m_a.get(x - 2))

                    weigh(0)
                    for x in range(E):
                        if x + 1 < E:
                            weigh(x + 1)
                        pe.wait(m_w[x])
                        for c in range(C):
                            for i in range(C):
                                last = nc.tensor.matmul(acc[c][:, :], w12[:, x, i, c * P:(c + 1) * P],
                                                        ye[x % 2][:, i, :], start=False,
                                                        stop=(x == E - 1 and i == C - 1))
                        m_a[x] = pe.count.mark(last)
                        yield
                    r = ye[0]
                    for c in range(C):
                        m = free[2 + c] = dve(lambda e: e.tensor_tensor(r[:, c, :], yv[c], acc[c][:, :], ALU.add),
                                              m_a[E - 1])

                    def context():
                        for c in range(C):
                            mk = matmul(bk[2 + c][:, :], [(w1k[:, i, c * P:(c + 1) * P], cb[:, i, :])
                                                          for i in range(C)], c_in, free[2 + c])
                            free[2 + c] = act(lambda e: e.activation(k1[:, c, :], bk[2 + c][:, :], ACT.Identity,
                                                                     bias=col("L1bk", c)), mk)
                            yield
                        for kt in range(KT):
                            k = 2 + kt % 2
                            mv = matmul(bk[k][:, 0:D], [(cb[:, i, kt * P:(kt + 1) * P], w1v[:, i, :])
                                                        for i in range(C)], free[k])
                            free[k] = act(lambda e: e.activation(v1[:, kt, :], bk[k][:, 0:D], ACT.Copy), mv)
                            yield

                    context_part = context()
                    m_y = []
                    for _ in layernorm_steps(lambda c: r[:, c, :], lambda c: yn[:, c, :], sq, std, bk[0][:, :],
                                             bk[1][:, :], [m], [m_w[E - 1]], lambda c: col("ln2_g", c),
                                             lambda c: col("ln2_b", c), out=m_y):
                        next(context_part, None)
                        yield
                    dve.wait(x_in)
                    for c in range(C):
                        m = dve(lambda e: e.scalar_tensor_tensor(xb[:, c, :], yn[:, c, :], TF0, xb[:, c, :],
                                                                 ALU.mult, ALU.add), m_y[c])
                    m_n = []
                    for _ in layernorm_steps(lambda c: xb[:, c, :], lambda c: yn[:, c, :], sq, std, bk[0][:, :],
                                             bk[1][:, :], [m], [], out=m_n):
                        next(context_part, None)
                        yield
                    for _ in context_part:
                        pass
                    for c in range(C):
                        mq = matmul(bk[c][:, :], [(w1q[:, i, c * P:(c + 1) * P], yn[:, i, :]) for i in range(C)],
                                    *m_n)
                        m_q = dve(lambda e: e.tensor_scalar(q1[:, c, :], bk[c][:, :], col("L1bq", c), D ** -0.5,
                                                            ALU.add, ALU.mult), mq)
                    m_v = act.count.now()
                    yield
                    m_S, m_e, m_tr, m_ev, m_p = {}, {}, {}, {}, {}
                    p1 = cb

                    def softmax(t):
                        s = t % 2
                        m_S[t] = matmul(bk[s][:, :], [(q1[:, c, t * P:(t + 1) * P], k1[:, c, :])
                                                      for c in range(C)], m_q, m_v, m_e.get(t - 2))
                        m = dve(lambda e: e.tensor_reduce(st1[:, s, 0:1], bk[s][:, :], AXIS_X, ALU.max), m_S[t],
                                m_e.get(t - 2))
                        m = dve(lambda e: e.tensor_scalar(st1[:, s, 1:2], st1[:, s, 0:1], -1.0, None, ALU.mult), m)
                        m_e[t] = act(lambda e: e.activation(p1[:, s, :], bk[s][:, :], ACT.Exp,
                                                            bias=st1[:, s, 1:2], accum_out=st1[:, s, 2:3]),
                                     m, m_tr.get(t - 2))

                    def normalise(t):
                        s = t % 2
                        m = dve(lambda e: e.reciprocal(st1[:, s, 3:4], st1[:, s, 2:3]), m_e[t])
                        m_p[t] = dve(lambda e: e.tensor_scalar(p1[:, s, :], p1[:, s, :], st1[:, s, 3:4], None,
                                                               ALU.mult), m)

                    def turn(t):
                        s = t % 2
                        pe.wait(m_p[t], free[2 + s])
                        for kt in range(KT):
                            last = nc.tensor.transpose(bk[2 + s][:, kt * P:(kt + 1) * P],
                                                       p1[:, s, kt * P:(kt + 1) * P], ident[:, :])
                        m_tr[t] = pe.count.mark(last)
                        m_ev[t] = free[2 + s] = act(lambda e: e.activation(
                            pT1[:, :, t * P:(t + 1) * P],
                            bk[2 + s][:, :].rearrange("p (k i) -> p k i", k=KT), ACT.Copy), m_tr[t])

                    for t in range(QB):
                        softmax(t)
                        yield
                        normalise(t)
                        if t:
                            turn(t - 1)
                        yield
                    turn(QB - 1)
                    yield
                    zT = sq
                    for c in range(C):
                        m = matmul(bk[c][:, :], [(v1[:, kt, c * P:(c + 1) * P], pT1[:, kt, :])
                                                 for kt in range(KT)], m_ev[QB - 1], m_e[QB - 2 + c])
                        m_zz = dve(lambda e: e.tensor_scalar(zT[:, c, :], bk[c][:, :], col("L1bv", c), None,
                                                             ALU.add), m)
                        yield
                    x3 = st.x3
                    for c in range(C):
                        m = matmul(bk[2 + c][:, :], [(wls[:, i, c * P:(c + 1) * P], zT[:, i, :])
                                                     for i in range(C)], m_zz, free[2 + c])
                        m = dve(lambda e: e.tensor_scalar(yn[:, c, :], bk[2 + c][:, :], col("L1bl", c), TX1,
                                                          ALU.add, ALU.mult), m)
                        free[2 + c] = m
                        m_x3 = dve(lambda e: e.tensor_tensor(x3[:, c, :], xb[:, c, :], yn[:, c, :], ALU.add), m,
                                   st.spikes_done)
                    yield
                    m_n = []
                    yield from layernorm_steps(lambda c: x3[:, c, :], lambda c: yn[:, c, :], sq, std, bk[0][:, :],
                                               bk[1][:, :], [m_x3], [], out=m_n)
                    hb, m_h, m_pr = st.wide, {}, {}

                    def project(i):
                        pe.wait(m_h[i], free[2], free[3])
                        for c in range(C):
                            last = nc.tensor.matmul(bk[2 + c][:, :], wpr[:, i, c * P:(c + 1) * P], hb[:, i % 4, :],
                                                    start=(i == 0), stop=(i == FF // P - 1))
                        m_pr[i] = pe.count.mark(last)

                    for i in range(FF // P):
                        k = i % 2
                        m = matmul(bk[k][:, :], [(wfc[:, c, i * P:(i + 1) * P], yn[:, c, :]) for c in range(C)],
                                   *m_n, m_h.get(i - 2))
                        m = act(lambda e: e.activation(hb[:, i % 4, :], bk[k][:, :], ACT.Relu), m,
                                m_pr.get(i - 4))
                        m_h[i] = dve(lambda e: e.tensor_tensor(hb[:, i % 4, :], hb[:, i % 4, :], hb[:, i % 4, :],
                                                               ALU.mult), m)
                        if i:
                            project(i - 1)
                        yield
                    project(FF // P - 1)
                    for c in range(C):
                        dve(lambda e: e.tensor_copy(st.y[:, c, :], bk[2 + c][:, :]), m_pr[FF // P - 1])

                def spikes(st, b):
                    y, mem = flat(st.y), flat(st.mem)
                    now = dve.count.now
                    dve(lambda e: e.tensor_scalar(cnt[:, :], y, 1.0, None, ALU.is_gt), now())
                    for n in range(4):
                        old = mem if n else y
                        dve(lambda e: e.scalar_tensor_tensor(tmp[:, :], old, 0.9, y, ALU.mult, ALU.add), now())
                        yield
                        dve(lambda e: e.scalar_tensor_tensor(mem, old, 1.0, tmp[:, :], ALU.is_gt, ALU.subtract,
                                                             reverse1=True), now())
                        yield
                        dve(lambda e: e.scalar_tensor_tensor(cnt[:, :], mem, 1.0, cnt[:, :], ALU.is_gt, ALU.add),
                            now())
                        yield
                    m = dve(lambda e: e.scalar_tensor_tensor(flat(st.x3), cnt[:, :], tf5[:, 0:1], flat(st.x3),
                                                             ALU.mult, ALU.add), now())
                    st.spikes_done = load(f"out{st.n}", o("out")[bass.ds(b, 1)].rearrange("o c p s -> p (o c) s"),
                                          st.x3[:, :, :], m)

                def first_of(n):
                    b = 2 * n
                    yield from layer1(streams[0], b)
                    yield from spikes(streams[0], b)

                def pair(n, done):
                    first, second = streams
                    a, b = first_of(n), layer1(second, 2 * n + 1)
                    sp = later(SPIKE_DELAY, spikes(second, 2 * done + 1)) if done is not None else iter(())
                    for _ in range(LAG):
                        next(a)
                        next(sp, None)
                    interleave((a, 1), (b, 1), (sp, 1))
                    for st in streams:
                        if st.spikes_done is not None:
                            nc.sync.wait_ge(st.spikes_done.sem, st.spikes_done.value)
                            nc.sync.sem_inc(written, 1)
                        st.spikes_done = None
                    barrier()

                pair(0, None)
                with loop("layer1", B // 2 - 1) as n:
                    pair(n + 1, n)
                for _ in spikes(streams[1], B - 1):
                    pass
                m = streams[1].spikes_done
                nc.sync.wait_ge(m.sem, m.value)
                barrier()


HIGH_ACT = (0, 4)
LOW_DVE = (0, 4)
HEAD_START, TERM_STEPS = 5, 3
SPIKE_DELAY = 14
MHA_LAG = 1
LAG = 5
COLS = [(n, c) for n, k in (("bq", 8), ("bk", 8), ("bv", 8), ("bo", 2), ("b_in", 6), ("b_out", 2),
                            ("ln1_g", 2), ("ln1_b", 2), ("ln2_g", 2), ("ln2_b", 2), ("L1bq", 2), ("L1bk", 2),
                            ("L1bv", 2), ("L1bl", 2), ("pix_freq", 1), ("pix_phase", 1), ("sep_freq", 1), ("phase1", 1),
                            ("phase2", 1), ("a_high", 1), ("a_low", 1), ("b_high", 1), ("b_low", 1),
                            ("quarter", 1)) for c in range(k)]


def shape_constants():
    f = np.float32
    dims = [1.0, WAVE ** -0.5]
    p = np.arange(P)
    const = {"ident": np.eye(P, dtype=f), "fold": (p[:, None] % QT == np.arange(QT)).astype(f),
             "tri": (p[:, None] <= p[None, :]).astype(f),
             "rank": np.tile(np.arange(E, 0, -1, dtype=f), (P, 1)),
             "mask": np.where(p[:, None] % 16 == p[None, :] % 16, 0.0, MASKED).astype(f)}
    row, block = (p % 32) % SEP, (p % 32) // SEP
    used = (p % 32) < 3 * SEP
    trig = used & (row < 8)
    col = {}
    col["pix_freq"] = np.array([100.0 * dims[(i // 32) % 2] / (2 * math.pi) for i in p])
    col["pix_phase"] = np.where(p % 32 < QT, 0.0, 0.25)
    col["sep_freq"] = np.where(trig, [100.0 * dims[(r // 2) % 2] / (2 * math.pi) for r in row], 0.0)
    cos_row = row % 2 == 0
    col["phase1"] = np.where(used & cos_row, 0.25, 0.0)
    col["phase2"] = np.where(trig & ~cos_row, -0.25, 0.0)
    col["a_high"] = (used & (block != 1)).astype(f)
    col["a_low"] = (used & (block == 1)).astype(f)
    col["b_high"] = (used & (block != 2)).astype(f)
    col["b_low"] = (used & (block == 2)).astype(f)
    col["quarter"] = np.full(P, TURN / 4)
    sel = np.zeros((4, 2, P), f)
    for i in p:
        y = i // 64
        sel[y, 0, i] = sel[2 + y, 0, i] = 1.0
        if trig[i]:
            y = row[i] // 4
            sel[y, 1, i], sel[2 + y, 1, i] = -1.0, 1.0
    const["sel"] = sel
    return const, {k: np.asarray(v, f) for k, v in col.items()}


def kernel(**inputs):
    import concourse.bacc as bacc
    from concourse.bass_utils import run_bass_kernel_spmd

    v = {k: np.asarray(a) for k, a in inputs.items()}
    const, col = shape_constants()

    def chunks(a):
        return a.reshape(-1, P).T

    def features_first(a):
        return np.ascontiguousarray(a.transpose(0, 2, 1)).reshape(B, C, P, S)

    per_partition = {
        "bq": v["L0_xattn_bq"], "bk": v["L0_xattn_bk"], "bv": v["L0_xattn_bv"], "bo": v["L0_xattn_bo"],
        "b_in": v["L0_ffn_in_proj_b"], "b_out": v["L0_ffn_out_proj_b"], "ln1_g": v["L0_ffn_ln1_g"],
        "ln1_b": v["L0_ffn_ln1_b"], "ln2_g": v["L0_ffn_ln2_g"], "ln2_b": v["L0_ffn_ln2_b"],
        "L1bq": v["L1_xattn_bQ"], "L1bk": v["L1_xattn_bK"], "L1bv": v["L1_xattn_bV"], "L1bl": v["L1_xattn_bl"],
    }
    cols = np.empty((P, len(COLS)), np.float32)
    for k, (name, c) in enumerate(COLS):
        cols[:, k] = chunks(per_partition[name])[:, c] if name in per_partition else col[name]

    wg = v["L0_xattn_Wg"]
    feature = np.arange(P) // 32 + np.arange(P) % 32 // QT * 8
    rel_w = wg[:, feature].T
    sep_w = np.zeros((P, 2, QUADS), np.float32)
    for i in range(P):
        row = (i % 32) % SEP
        if i % 32 < 3 * SEP:
            heads = np.arange(QUADS) * 4 + i // 32
            if row < 8:
                sep_w[i, 0], sep_w[i, 1] = wg[heads, 12 + row // 2], wg[heads, 4 + row // 2]
            else:
                sep_w[i, 0] = v["L0_xattn_bg"][heads]
    boxes = v["fside_BxSx4_0"]
    by_query = boxes.reshape(B, NT, QT, 4)
    box_lo, box_hi = (np.stack([by_query[..., k + g // 4] for g in range(8)], 0)
                      .transpose(0, 3, 1, 2).reshape(P, B * NT) for k in (0, 2))
    b1x = np.zeros((E, P, FF // P, E), np.float32)
    for e in range(E):
        b1x[e, :, :, e] = v["L0_ffn_b1"][e].reshape(FF // P, P).T
    arrays = {
        **const, "cols": cols, "gates": np.concatenate([v["g_xattn"], v["g_ffn"]]),
        "xT": features_first(v["x"]), "ctxT": features_first(v["ctx_1024"]),
        "boxT": boxes.transpose(0, 2, 1), "box_lo": box_lo, "box_hi": box_hi, "rel_w": rel_w, "sep_w": sep_w,
        "wqT": v["L0_xattn_Wq"].T, "wkT": v["L0_xattn_Wk"].T, "wvT": v["L0_xattn_Wv"].T, "woT": v["L0_xattn_Wo"].T,
        "in_wT": v["L0_ffn_in_proj_w"].T, "out_wT": v["L0_ffn_out_proj_w"].T, "wg": v["L0_ffn_wg"],
        "w1T": v["L0_ffn_w1"].transpose(0, 2, 1), "w2": v["L0_ffn_w2"], "b1x": b1x, "b2": v["L0_ffn_b2"],
        "L1q": v["L1_xattn_WQ"].T, "L1k": v["L1_xattn_WK"].T, "L1v": v["L1_xattn_WV"].T,
        "wlT": v["L1_xattn_Wl"].T, "wfcT": v["L1_ffn_W_fc"].T, "wprT": v["L1_ffn_W_proj"].T,
    }
    arrays = {k: np.ascontiguousarray(a) for k, a in arrays.items()}

    def program(table):
        nc = bacc.Bacc("TRN2", target_bir_lowering=False, num_devices=1)
        io = {k: nc.dram_tensor("in_" + k, a.shape, mybir.dt.from_np(a.dtype), kind="ExternalInput").ap()
              for k, a in arrays.items()}
        io["out"] = nc.dram_tensor("out_0", (B, C, P, S), F32, kind="ExternalOutput").ap()
        build(nc, table, io)
        return nc

    table = {"per": {}, "names": {}, "new_per": {}, "new_names": {}}
    program(table)
    table["per"], table["names"] = table["new_per"], table["new_names"]
    table["new_per"], table["new_names"] = {}, {}
    nc = program(table)
    assert table["per"] == table["new_per"] and table["names"] == table["new_names"]
    r = run_bass_kernel_spmd(nc, [{"in_" + k: a for k, a in arrays.items()}], core_ids=[0])
    out = r.results[0]["out_0"]
    return np.ascontiguousarray(out.reshape(B, D, S).transpose(0, 2, 1))
```
